# Optimizing a Trainium2 kernel written in Bass

```python
import numpy as np
import jax
import jax.numpy as jnp

def _softmax(x, axis=-1):
    return jax.nn.softmax(x, axis=axis)

def _gelu(x):
    return jax.nn.gelu(x, approximate=True)

def _silu(x):
    return jax.nn.silu(x)

def _sigmoid(x):
    return jax.nn.sigmoid(x)

def _layernorm(x, axis=-1, eps=1e-05):
    m = jnp.mean(x, axis=axis, keepdims=True)
    v = jnp.var(x, axis=axis, keepdims=True)
    return (x - m) / jnp.sqrt(v + eps)

def _scatter_add(tgt, idx, src, axis=0):
    return tgt.at[idx].add(src)

def _segment_sum(src, seg, n):
    return jax.ops.segment_sum(src, seg, n)
kernel_name = 'mk_adaln_attn_ffn_d1_seqx_r8_472c04'

def setup_inputs(seed: int=0):
    np.random.seed(seed)
    _w = jnp.asarray

    def _rec_inputs():
        import jax
        import jax.numpy as jnp
        _rk = jax.random.key(seed)
        x = -0.0005207 + 1.001 * jax.random.normal(jax.random.fold_in(_rk, 1), (8, 256, 128), jnp.float32)
        _lenS = 256 - jax.random.randint(jax.random.fold_in(_rk, 7), (8,), 0, max(1, 256 // 4) + 1, jnp.int32)
        _lenS2 = 256 - jax.random.randint(jax.random.fold_in(_rk, 8), (8,), 0, max(1, 256 // 4) + 1, jnp.int32)
        fside_Bx8_0 = jax.random.uniform(jax.random.fold_in(_rk, 11), (8, 8), jnp.float32, 0.0, 0.556406)
        condB_sharedgateprob = jax.random.uniform(jax.random.fold_in(_rk, 12), (8,), jnp.float32, 0.0, 0.794948)
        itok_B_0_2 = jax.random.randint(jax.random.fold_in(_rk, 13), (8,), 0, 3, jnp.int32)
        return (x, fside_Bx8_0, condB_sharedgateprob, itok_B_0_2)
    x, fside_Bx8_0, condB_sharedgateprob, itok_B_0_2 = _rec_inputs()

    def _L0_cond_setup():
        import jax, jax.numpy as jnp
        import numpy as np
        E, B, S, D, F = (8, 2, 128, 128, 512)
        key = jax.random.key(seed)
        ks = jax.random.split(key, 9)
        sc_d = 1.0 / np.sqrt(D)
        sc_f = 1.0 / np.sqrt(F)
        hidden_states = jax.random.normal(ks[0], (B, S, D), dtype=jnp.float32)
        gating_probs = jax.nn.softmax(jax.random.normal(ks[1], (B, E), dtype=jnp.float32), axis=-1)
        shared_gate_prob = jax.nn.sigmoid(jax.random.normal(ks[2], (B, 1), dtype=jnp.float32))
        Wg = jax.random.normal(ks[3], (E, D, F), dtype=jnp.float32) * sc_d
        Wu = jax.random.normal(ks[4], (E, D, F), dtype=jnp.float32) * sc_d
        Wd = jax.random.normal(ks[5], (E, F, D), dtype=jnp.float32) * sc_f
        Sg = jax.random.normal(ks[6], (D, F), dtype=jnp.float32) * sc_d
        Su = jax.random.normal(ks[7], (D, F), dtype=jnp.float32) * sc_d
        Sd = jax.random.normal(ks[8], (F, D), dtype=jnp.float32) * sc_f
        return {'hidden_states': hidden_states, 'gating_probs': gating_probs, 'shared_gate_prob': shared_gate_prob, 'Wg': Wg, 'Wu': Wu, 'Wd': Wd, 'Sg': Sg, 'Su': Su, 'Sd': Sd}
    _L0_cond_all = _L0_cond_setup()
    _L0_cond_in = {k: v for k, v in _L0_cond_all.items() if k in ('Wg', 'Wu', 'Wd', 'Sg', 'Su', 'Sd')}
    del _L0_cond_all

    def _L0_attn_setup():
        import jax, jax.numpy as jnp
        import numpy as np
        D_MODEL = 128
        NUM_HEADS = 16
        HEAD_DIM = D_MODEL // NUM_HEADS
        LN_EPS = 0.001
        key = jax.random.key(seed)
        ks = jax.random.split(key, 10)
        B, T = (2, 256)
        s = 1.0 / np.sqrt(D_MODEL)
        return {'x': jax.random.normal(ks[0], (B, T, D_MODEL), dtype=jnp.float32), 'Wq': jax.random.normal(ks[1], (D_MODEL, D_MODEL), dtype=jnp.float32) * s, 'Wk': jax.random.normal(ks[2], (D_MODEL, D_MODEL), dtype=jnp.float32) * s, 'Wv': jax.random.normal(ks[3], (D_MODEL, D_MODEL), dtype=jnp.float32) * s, 'Wg': jax.random.normal(ks[4], (D_MODEL, D_MODEL), dtype=jnp.float32) * s, 'bg': jnp.zeros((D_MODEL,), dtype=jnp.float32), 'Wo': jax.random.normal(ks[5], (D_MODEL, D_MODEL), dtype=jnp.float32) * s, 'bo': jnp.zeros((D_MODEL,), dtype=jnp.float32), 'ln_gamma': jnp.ones((D_MODEL,), dtype=jnp.float32), 'ln_beta': jnp.zeros((D_MODEL,), dtype=jnp.float32)}
    _L0_attn_all = _L0_attn_setup()
    _L0_attn_in = {k: v for k, v in _L0_attn_all.items() if k in ('Wq', 'Wk', 'Wv', 'Wg', 'bg', 'Wo', 'bo', 'ln_gamma', 'ln_beta')}
    del _L0_attn_all

    def _L0_cond2_setup():
        import jax, jax.numpy as jnp
        import numpy as np
        NEG_INF = -1e+30
        key = jax.random.key(seed)
        k1, k2, k3, k4, k5 = jax.random.split(key, 5)
        B, S, D, A = (16, 128, 128, 32)
        hidden = jax.random.normal(k1, (B, S, D), dtype=jnp.float32)
        W1 = jax.random.normal(k2, (D, A), dtype=jnp.float32) / np.sqrt(D)
        b1 = jax.random.normal(k3, (A,), dtype=jnp.float32) * 0.01
        v = jax.random.normal(k4, (A,), dtype=jnp.float32) / np.sqrt(A)
        prompt_type_ids = jax.random.randint(k5, (B,), 0, 3, dtype=jnp.int32)
        return {'hidden': hidden, 'W1': W1, 'b1': b1, 'v': v, 'prompt_type_ids': prompt_type_ids}
    _L0_cond2_all = _L0_cond2_setup()
    _L0_cond2_in = {k: v for k, v in _L0_cond2_all.items() if k in ('W1', 'b1', 'v')}
    del _L0_cond2_all

    def _L0_ffn_setup():
        import jax, jax.numpy as jnp
        import numpy as np
        H = 16
        E = 8
        EPS = 1e-05

        def _layernorm(x, g, b):
            mu = jnp.mean(x, axis=-1, keepdims=True)
            var = jnp.mean(jnp.square(x - mu), axis=-1, keepdims=True)
            return (x - mu) * jax.lax.rsqrt(var + EPS) * g + b
        key = jax.random.key(seed)
        T, B, C = (128, 8, 128)
        ks = jax.random.split(key, 12)
        s = 0.02
        return {'x': jax.random.normal(ks[0], (T, B, C), jnp.float32), 'in_proj_w': jax.random.normal(ks[1], (3 * C, C), jnp.float32) * s, 'in_proj_b': jnp.zeros((3 * C,), jnp.float32), 'out_w': jax.random.normal(ks[2], (C, C), jnp.float32) * s, 'out_b': jnp.zeros((C,), jnp.float32), 'ln1_g': jnp.ones((C,), jnp.float32), 'ln1_b': jnp.zeros((C,), jnp.float32), 'router_w': jax.random.normal(ks[3], (E, C), jnp.float32) * s, 'router_b': jnp.zeros((E,), jnp.float32), 'w1': jax.random.normal(ks[4], (E, C, C), jnp.float32) * s, 'b1': jnp.zeros((E, C), jnp.float32), 'w2': jax.random.normal(ks[5], (E, C, C), jnp.float32) * s, 'b2': jnp.zeros((E, C), jnp.float32), 'ln2_g': jnp.ones((C,), jnp.float32), 'ln2_b': jnp.zeros((C,), jnp.float32)}
    _L0_ffn_all = _L0_ffn_setup()
    _L0_ffn_in = {k: v for k, v in _L0_ffn_all.items() if k in ('in_proj_w', 'in_proj_b', 'out_w', 'out_b', 'ln1_g', 'ln1_b', 'router_w', 'router_b', 'w1', 'b1', 'w2', 'b2', 'ln2_g', 'ln2_b')}
    del _L0_ffn_all
    return {'x': x, 'fside_Bx8_0': fside_Bx8_0, 'condB_sharedgateprob': condB_sharedgateprob, 'itok_B_0_2': itok_B_0_2, 'L0_cond_Wg': _L0_cond_in['Wg'], 'L0_cond_Wu': _L0_cond_in['Wu'], 'L0_cond_Wd': _L0_cond_in['Wd'], 'L0_cond_Sg': _L0_cond_in['Sg'], 'L0_cond_Su': _L0_cond_in['Su'], 'L0_cond_Sd': _L0_cond_in['Sd'], 'L0_attn_Wq': _L0_attn_in['Wq'], 'L0_attn_Wk': _L0_attn_in['Wk'], 'L0_attn_Wv': _L0_attn_in['Wv'], 'L0_attn_Wg': _L0_attn_in['Wg'], 'L0_attn_bg': _L0_attn_in['bg'], 'L0_attn_Wo': _L0_attn_in['Wo'], 'L0_attn_bo': _L0_attn_in['bo'], 'L0_attn_ln_gamma': _L0_attn_in['ln_gamma'], 'L0_attn_ln_beta': _L0_attn_in['ln_beta'], 'L0_cond2_W1': _L0_cond2_in['W1'], 'L0_cond2_b1': _L0_cond2_in['b1'], 'L0_cond2_v': _L0_cond2_in['v'], 'L0_ffn_in_proj_w': _L0_ffn_in['in_proj_w'], 'L0_ffn_in_proj_b': _L0_ffn_in['in_proj_b'], 'L0_ffn_out_w': _L0_ffn_in['out_w'], 'L0_ffn_out_b': _L0_ffn_in['out_b'], 'L0_ffn_ln1_g': _L0_ffn_in['ln1_g'], 'L0_ffn_ln1_b': _L0_ffn_in['ln1_b'], 'L0_ffn_router_w': _L0_ffn_in['router_w'], 'L0_ffn_router_b': _L0_ffn_in['router_b'], 'L0_ffn_w1': _L0_ffn_in['w1'], 'L0_ffn_b1': _L0_ffn_in['b1'], 'L0_ffn_w2': _L0_ffn_in['w2'], 'L0_ffn_b2': _L0_ffn_in['b2'], 'L0_ffn_ln2_g': _L0_ffn_in['ln2_g'], 'L0_ffn_ln2_b': _L0_ffn_in['ln2_b']}

def reference(x, fside_Bx8_0, condB_sharedgateprob, itok_B_0_2, L0_cond_Wg, L0_cond_Wu, L0_cond_Wd, L0_cond_Sg, L0_cond_Su, L0_cond_Sd, L0_attn_Wq, L0_attn_Wk, L0_attn_Wv, L0_attn_Wg, L0_attn_bg, L0_attn_Wo, L0_attn_bo, L0_attn_ln_gamma, L0_attn_ln_beta, L0_cond2_W1, L0_cond2_b1, L0_cond2_v, L0_ffn_in_proj_w, L0_ffn_in_proj_b, L0_ffn_out_w, L0_ffn_out_b, L0_ffn_ln1_g, L0_ffn_ln1_b, L0_ffn_router_w, L0_ffn_router_b, L0_ffn_w1, L0_ffn_b1, L0_ffn_w2, L0_ffn_b2, L0_ffn_ln2_g, L0_ffn_ln2_b):
    import jax
    import jax.numpy as jnp

    def _L0_cond_ref(hidden_states, gating_probs, shared_gate_prob, Wg, Wu, Wd, Sg, Su, Sd):
        import jax, jax.numpy as jnp
        import numpy as np
        E, B, S, D, F = (8, 2, 128, 128, 512)
        h = hidden_states
        g = jnp.einsum('bsd,edf->ebsf', h, Wg)
        u = jnp.einsum('bsd,edf->ebsf', h, Wu)
        expert_outs = jnp.einsum('ebsf,efd->ebsd', jax.nn.silu(g) * u, Wd)
        expert_output = jnp.einsum('be,ebsd->bsd', gating_probs, expert_outs)
        shared = jnp.einsum('bsf,fd->bsd', jax.nn.silu(h @ Sg) * (h @ Su), Sd)
        sg = shared_gate_prob[:, :, None]
        return (1.0 - sg) * expert_output + sg * shared

    def _L0_attn_ref(x, Wq, Wk, Wv, Wg, bg, Wo, bo, ln_gamma, ln_beta):
        import jax, jax.numpy as jnp
        import numpy as np
        D_MODEL = 128
        NUM_HEADS = 16
        HEAD_DIM = D_MODEL // NUM_HEADS
        LN_EPS = 0.001
        B, T, D = x.shape
        H, dh = (NUM_HEADS, HEAD_DIM)

        def split_heads(z):
            return z.reshape(B, T, H, dh).transpose(0, 2, 1, 3)
        Q = split_heads(x @ Wq)
        K = split_heads(x @ Wk)
        V = split_heads(x @ Wv)
        G = jax.nn.swish(x @ Wg + bg)
        idx = jnp.arange(T, dtype=jnp.float32)
        diff = idx[:, None] - idx[None, :]
        causal = (diff >= 0).astype(jnp.float32)
        gammas = 1.0 - 2.0 ** (-5.0 - jnp.arange(H, dtype=jnp.float32))
        Dmask = gammas[:, None, None] ** jnp.maximum(diff, 0.0) * causal
        scale = float(dh) ** 0.5
        scores = jnp.einsum('bhtd,bhsd->bhts', Q, K) / scale
        ret = jnp.einsum('bhts,bhsd->bhtd', scores * Dmask[None], V)
        ret = ret.transpose(0, 2, 1, 3).reshape(B, T, D)
        mu = jnp.mean(ret, axis=-1, keepdims=True)
        var = jnp.mean(jnp.square(ret - mu), axis=-1, keepdims=True)
        ln = (ret - mu) / jnp.sqrt(var + LN_EPS) * ln_gamma + ln_beta
        return ln * G @ Wo + bo

    def _L0_cond2_ref(hidden, W1, b1, v, prompt_type_ids):
        import jax, jax.numpy as jnp
        import numpy as np
        NEG_INF = -1e+30
        B, S, D = hidden.shape
        attn_in = jnp.tanh(jnp.einsum('bsd,da->bsa', hidden, W1) + b1)
        scores = jnp.einsum('bsa,a->bs', attn_in, v)
        idx = jnp.arange(S)
        j = idx[:, None]
        l = idx[None, :]
        prefix_m = l <= j
        postfix_m = l >= j
        cloze_m = l != j
        pt = prompt_type_ids[:, None, None]
        mask = jnp.where(pt == 0, prefix_m[None], jnp.where(pt == 1, postfix_m[None], cloze_m[None]))
        masked_scores = jnp.where(mask, scores[:, None, :], NEG_INF)
        p = jax.nn.softmax(masked_scores, axis=-1)
        cnt = jnp.sum(mask, axis=-1).astype(hidden.dtype)
        pooled = jnp.einsum('bjl,bld->bjd', p, hidden) / cnt[..., None]
        return pooled

    def _L0_ffn_ref(x, in_proj_w, in_proj_b, out_w, out_b, ln1_g, ln1_b, router_w, router_b, w1, b1, w2, b2, ln2_g, ln2_b):
        import jax, jax.numpy as jnp
        import numpy as np
        H = 16
        E = 8
        EPS = 1e-05

        def _layernorm(x, g, b):
            mu = jnp.mean(x, axis=-1, keepdims=True)
            var = jnp.mean(jnp.square(x - mu), axis=-1, keepdims=True)
            return (x - mu) * jax.lax.rsqrt(var + EPS) * g + b
        T, B, C = x.shape
        D = C // H
        qkv = x @ in_proj_w.T + in_proj_b
        q, k, v = jnp.split(qkv, 3, axis=-1)
        q = q.reshape(T, B, H, D)
        k = k.reshape(T, B, H, D)
        v = v.reshape(T, B, H, D)
        scale = 1.0 / np.sqrt(D).astype(np.float32)
        scores = jnp.einsum('tbhd,sbhd->bhts', q, k) * scale
        attn = jax.nn.softmax(scores, axis=-1)
        ctx = jnp.einsum('bhts,sbhd->tbhd', attn, v).reshape(T, B, C)
        attn_out = ctx @ out_w.T + out_b
        h = _layernorm(x + attn_out, ln1_g, ln1_b)
        flat = h.reshape(-1, C)
        logits = flat @ router_w.T + router_b
        probs = jax.nn.softmax(logits, axis=-1)
        _, top_i = jax.lax.top_k(probs, 2)
        assign = jnp.max(top_i, axis=-1)
        out = jnp.zeros_like(flat)
        for e in range(E):
            he = jax.nn.gelu(flat @ w1[e].T + b1[e], approximate=False)
            oe = he @ w2[e].T + b2[e]
            out = jnp.where((assign == e)[:, None], oe, out)
        moe_out = out.reshape(T, B, C)
        return _layernorm(h + moe_out, ln2_g, ln2_b)
    x = x + _L0_attn_ref(_L0_cond_ref(x, fside_Bx8_0, condB_sharedgateprob[:, None], L0_cond_Wg, L0_cond_Wu, L0_cond_Wd, L0_cond_Sg, L0_cond_Su, L0_cond_Sd), L0_attn_Wq, L0_attn_Wk, L0_attn_Wv, L0_attn_Wg, L0_attn_bg, L0_attn_Wo, L0_attn_bo, L0_attn_ln_gamma, L0_attn_ln_beta)
    x = x + _L0_ffn_ref(_L0_cond2_ref(x, L0_cond2_W1, L0_cond2_b1, L0_cond2_v, itok_B_0_2), L0_ffn_in_proj_w, L0_ffn_in_proj_b, L0_ffn_out_w, L0_ffn_out_b, L0_ffn_ln1_g, L0_ffn_ln1_b, L0_ffn_router_w, L0_ffn_router_b, L0_ffn_w1, L0_ffn_b1, L0_ffn_w2, L0_ffn_b2, L0_ffn_ln2_g, L0_ffn_ln2_b)
    return x

_drawn_inputs = setup_inputs


def setup_inputs(seed=0):
    import zlib

    import numpy as np

    out = dict(_drawn_inputs(seed))
    spreads = {'L0_attn_bg': (0.0, 0.1),
     'L0_attn_bo': (0.0, 0.1),
     'L0_attn_ln_gamma': (1.0, 0.2),
     'L0_attn_ln_beta': (0.0, 0.44),
     'L0_ffn_in_proj_b': (0.0, 0.1),
     'L0_ffn_out_b': (0.0, 0.1),
     'L0_ffn_ln1_g': (1.0, 0.2),
     'L0_ffn_ln1_b': (0.0, 0.1),
     'L0_ffn_router_b': (0.0, 0.316),
     'L0_ffn_b1': (0.0, 0.8),
     'L0_ffn_b2': (0.0, 0.1),
     'L0_ffn_ln2_g': (1.0, 0.2),
     'L0_ffn_ln2_b': (0.0, 0.1)}
    factors = {'L0_cond2_b1': 8.0, 'L0_ffn_in_proj_w': 7.963, 'L0_ffn_w1': 3.104}
    for name, (base, spread) in spreads.items():
        noise = np.random.default_rng([zlib.crc32(name.encode()), seed]).standard_normal(out[name].shape)
        drawn = base * np.exp(spread * noise) if base else spread * noise
        out[name] = jnp.asarray(drawn.astype(out[name].dtype))
    for name, factor in factors.items():
        out[name] = (out[name] * factor).astype(out[name].dtype)
    return out
```

```python
from contextlib import ExitStack

import numpy as np

import concourse.bass as bass
from concourse import mybir

ALU = mybir.AluOpType
ACT = mybir.ActivationFunctionType
AX = mybir.AxisListType
F32 = mybir.dt.float32
F32R = mybir.dt.float32r
BF16 = mybir.dt.bfloat16
I32 = mybir.dt.int32
U16 = mybir.dt.uint16

P = 128
B = 8
T = 256
JT = T // P
F = 512
NE = 9
UNITS = 2 * NE
H = 16
DH = P // H
E = 8
A = 32
QKV = 3 * P
GROUPS = 4
GT = 4
GC = GT * P
NEWTON = 3
RSTEPS = 3 + 3 * NEWTON
RET_EPS = 1e-3
LN_EPS = 1e-5
HEAD_SCALE = float(DH) ** -0.5
BIG = 1e30
MAGIC = 1597463007.0

WQ, WK, WV, WGATE, WO, WPOOL, WIN, WOUT, WROUTE, WEND = np.cumsum([0, P, P, P, P, P, A, QKV, P, E]).tolist()
C_BG, C_BO, C_GAMMA, C_BETA, C_B1 = 0, 1, 2, 3, 4
R_INB, R_OUTB, R_G1, R_B1, R_G2, R_B2, R_RB, R_END = np.cumsum([0, QKV, P, P, P, P, P, E]).tolist()
K_DECAY, K_CNT, K_IDX, K_TRI, K_END = np.cumsum([0, 2 * T, 3 * JT, E, E * E]).tolist()


def build(nc, xT, experts, proj, moe_w1, moe_w2, cols, small, rows, moe_b2, fside, prob, itok,
          spread, gather, ident_in, masks, consts, big, out):
    qkvp_dram = nc.dram_tensor("qkvp_scratch", (P, B, JT, QKV + P), F32, kind="Internal").ap()
    x2_dram = nc.dram_tensor("x2_scratch", (P, B, T), F32, kind="Internal").ap()

    with ExitStack() as ctx:
        names = set()

        def sem(name):
            return ctx.enter_context(nc.semaphore(name))

        def bank(name):
            return ctx.enter_context(nc.psum_tensor(name, [P, 512], F32))

        place = {"at": (nc.sbuf_base + 63) // 64 * 64}

        def sb(name, cols_, dt=F32):
            assert name not in names
            names.add(name)
            size = cols_ * (2 if dt == BF16 else 4)
            t = nc.alloc_sbuf_tensor_at(name, [P, cols_], dt, offset=place["at"])
            place["at"] += (size + 63) // 64 * 64
            return t

        ident = sb("ident", P)
        row_bc = sb("row_bc", R_END)
        col = sb("col", C_B1 + E)
        const = sb("const", K_END)
        projw = sb("projw", WEND)

        weights_at = place["at"]
        w_hi = sb("w_hi", NE * 3 * F, F32R)
        w_lo = sb("w_lo", NE * 3 * F, F32R)
        weights_end = place["at"]
        raw_at = place["at"]
        w_raw = sb("w_raw", 2 * 3 * F)
        raw_end = place["at"]
        place["at"] = raw_at
        kv = sb("kv", 2 * 2 * T)
        state = sb("state", DH * T)
        assert place["at"] <= raw_end
        place["at"] = raw_end
        x_sb = sb("x_sb", (B + 1) * T)
        x_hi = sb("x_hi", 2 * T, F32R)
        x_lo = sb("x_lo", 2 * T, F32R)
        masks_sb = sb("masks_sb", 3 * JT * T, BF16)
        mask_now = sb("mask_now", JT * T, BF16)
        mask_part = sb("mask_part", JT * T, BF16)
        spread_r = sb("spread_r", DH * P, F32R)
        gather_c = sb("gather_c", DH * P)
        h_hi = sb("h_hi", 2 * 2 * T, F32R)
        h_lo = sb("h_lo", 2 * 2 * T, F32R)
        hidden = sb("hidden", 2 * 2 * T)
        small_at = place["at"]
        p_hi = sb("p_hi", 4 * P, F32R)
        p_lo = sb("p_lo", 4 * P, F32R)
        ones = sb("ones", P)
        mean_col = sb("mean_col", 1)
        coef = sb("coef", B * NE)
        cnt = sb("cnt", B * JT)
        fs_bc = sb("fs_bc", B * E)
        pr_bc = sb("pr_bc", B)
        it_bc = sb("it_bc", B, I32)
        itf = sb("itf", B)
        sel_u = sb("sel_u", B)
        sel_l = sb("sel_l", B)
        sel_d = sb("sel_d", B)
        small_sb = sb("small_sb", 2)
        nv_rep = sb("nv_rep", P)
        chain_at = place["at"]
        c_hi = sb("c_hi", T, F32R)
        c_lo = sb("c_lo", T, F32R)
        kT = sb("kT", T)
        v_hi = sb("v_hi", T, F32R)
        v_lo = sb("v_lo", T, F32R)
        qT = sb("qT", T)
        gT = sb("gT", T)
        gammaT = sb("gammaT", T)
        betaT = sb("betaT", T)
        cenT = sb("cenT", T)
        sqT = sb("sqT", T)
        diag = sb("diag", JT * P)
        scaledT = sb("scaledT", T)
        lnT = sb("lnT", T)
        x2T = sb("x2T", T)
        x2n = sb("x2n", T)
        atT = sb("atT", T)
        mk = sb("mk", JT * T)
        ex = sb("ex", JT * T)
        pT = sb("pT", JT * T)
        plT = sb("plT", T)
        stage = sb("stage", JT * (QKV + P))
        nw = sb("nw", 8 * JT)
        nwi = sb("nwi", 2 * JT, I32)
        mxn = sb("mxn", JT)
        ssum = sb("ssum", JT)
        cnt_now = sb("cnt_now", JT)
        rn = sb("rn", 2 * JT)
        chain_end = place["at"]
        assert chain_end <= nc.sbuf_usable_end, (chain_end, nc.sbuf_usable_end)
        place["at"] = chain_at
        spread_raw = sb("spread_raw", DH * P)
        assert place["at"] <= chain_end

        W = QKV + P
        place["at"] = weights_at
        att = [sb(f"att{j}", B * W) for j in range(JT)]
        x2_all = sb("x2_all", B * T)
        w1_raw = sb("w1_raw", E * P)
        w1_hi = sb("w1_hi", E * P, F32R)
        w1_lo = sb("w1_lo", E * P, F32R)
        w2_sb = sb("w2_sb", E * P)
        b2_sb = sb("b2_sb", P)
        big_b = sb("big_b", E * P, BF16)
        ring_dve = sb("ring_dve", 2 * B * P)
        ring_pool = sb("ring_pool", 2 * B * P)
        sc = sb("sc", JT * B * P)
        smx = sb("smx", GROUPS * GT * H)
        ssm = sb("ssm", GROUPS * GT * H)
        resid = sb("resid", GROUPS * GC)
        hn = sb("hn", GROUPS * GC)
        assert place["at"] <= weights_end, (place["at"], weights_end)
        place["at"] = raw_at
        atn = sb("atn", 2 * GC)
        ctxT = sb("ctxT", 2 * GC)
        stats = sb("stats", GT * 6)
        aggr = sb("aggr", GT * 2)
        nf = sb("nf", 4 * GT)
        nfi = sb("nfi", 2 * GT, I32)
        logit = sb("logit", GT * E)
        r_gt = sb("r_gt", GT * E * E)
        r_eq = sb("r_eq", GT * E * E)
        r_rank = sb("r_rank", GT * E)
        r_val = sb("r_val", GT * E)
        r_max = sb("r_max", GT)
        onehot = sb("onehot", GT * E)
        assert place["at"] <= raw_end
        place["at"] = raw_end
        hT = sb("hT", 2 * GC)
        hT_hi = sb("hT_hi", 2 * GC, F32R)
        hT_lo = sb("hT_lo", 2 * GC, F32R)
        he = sb("he", 2 * GC)
        zf = sb("zf", 2 * GC)
        ohT = sb("ohT", 2 * GC)
        ohT_b = sb("ohT_b", 2 * GC, BF16)
        assert place["at"] <= small_at, (place["at"], small_at)

        pg = [bank("pg0"), bank("pg1")]
        pu = [bank("pu0"), bank("pu1")]
        acc = bank("acc")
        r0, r1, r2 = bank("r0"), bank("r1"), bank("r2")

        ld_x0, ld_x, ld_small, ld_proj, ld_const, ld_masks, ld_spread = (
            sem(n) for n in ("ld_x0", "ld_x", "ld_small", "ld_proj", "ld_const", "ld_masks", "ld_spread"))
        ld_w = [sem(f"ld_w{i}") for i in range(NE)]
        w_hi_done, w_lo_done, w_lo_pool, wd_hi_done, wd_lo_pool = (
            sem(n) for n in ("w_hi_done", "w_lo_done", "w_lo_pool", "wd_hi_done", "wd_lo_pool"))
        x_hi_done, x_lo_done = sem("x_hi_done"), sem("x_lo_done")
        p_hi_done, p_lo_done, spread_done = sem("p_hi_done"), sem("p_lo_done"), sem("spread_done")
        setup_step, setup_dve_step, kinds_done, route_gt = (
            sem(n) for n in ("setup_step", "setup_dve_step", "kinds_done", "route_gt"))
        g_ready, u_ready, silu_done, h_done = sem("g_ready"), sem("u_ready"), sem("silu_done"), sem("h_done")
        hi_done, lo_done, down_done = sem("hi_done"), sem("lo_done"), sem("down_done")
        cond_hi, cond_lo, kvqg_ready = sem("cond_hi"), sem("cond_lo"), sem("kvqg_ready")
        v_hi_done, v_lo_done, k_done, q_done, gate_done = (
            sem(n) for n in ("v_hi_done", "v_lo_done", "k_done", "q_done", "gate_done"))
        gammaT_done, betaT_done, scaled_done = sem("gammaT_done"), sem("betaT_done"), sem("scaled_done")
        vb_ready, kv_done, state_done, qs_done = sem("vb_ready"), sem("kv_done"), sem("state_done"), sem("qs_done")
        cen_ready, cen_done, sq_done, var_ready = sem("cen_ready"), sem("cen_done"), sem("sq_done"), sem("var_ready")
        rstd_step, bc_ready, ln_step, wo_ready = sem("rstd_step"), sem("bc_ready"), sem("ln_step"), sem("wo_ready")
        x2_done, x2t_ready, pre_ready, at_done = sem("x2_done"), sem("x2t_ready"), sem("pre_ready"), sem("at_done")
        x2n_done, s_ready, masked, exp_done = sem("x2n_done"), sem("s_ready"), sem("masked"), sem("exp_done")
        pt_ready, pt_done, pooled_ready, plT_done = (
            sem(n) for n in ("pt_ready", "pt_done", "pooled_ready", "plT_done"))
        rn_step, pooled_done, qkv_ready, qkv_done = sem("rn_step"), sem("pooled_done"), sem("qkv_ready"), sem("qkv_done")
        x2n_sent, qkv_sent, mask_now_done, mask_step, cnt_done = (
            sem(n) for n in ("x2n_sent", "qkv_sent", "mask_now_done", "mask_step", "cnt_done"))
        ld_f, ld_x2, ld_att = sem("ld_f"), sem("ld_x2"), [sem(f"ld_att{j}") for j in range(JT)]
        x2_kept, w1_hi_done, w1_lo_done = sem("x2_kept"), sem("w1_hi_done"), sem("w1_lo_done")
        prod_dve, sum_dve, prod_pool, read_pool, sum_pool, tree_pool = (
            sem(n) for n in ("prod_dve", "sum_dve", "prod_pool", "read_pool", "sum_pool", "tree_pool"))
        soft_step, norm_step, fexp_done, p_done, resid_done = (
            sem(n) for n in ("soft_step", "norm_step", "fexp_done", "p_done", "resid_done"))
        atT_ready, ctx_done, proj_ready, y_done = sem("atT_ready"), sem("ctx_done"), sem("proj_ready"), sem("y_done")
        stat_step, h_step, hT_ready, hT_done, hT_hi_done, hT_lo_done = (
            sem(n) for n in ("stat_step", "h_step", "hT_ready", "hT_done", "hT_hi_done", "hT_lo_done"))
        logit_ready, route_step, onehot_done = sem("logit_ready"), sem("route_step"), sem("onehot_done")
        ohT_ready, ohT_done, fpre_ready, gelu_done = (
            sem(n) for n in ("ohT_ready", "ohT_done", "fpre_ready", "gelu_done"))
        he_used, z_done, fin_step, fin_done = (sem(n) for n in ("he_used", "z_done", "fin_step", "fin_done"))
        out_sent = [sem(f"out_sent{i}") for i in range(2)]

        block = ctx.enter_context(nc.Block())

        def w_part(tile, e, kind, c):
            at = (e * 3 + kind) * F + c * P
            return tile[:, at:at + P]

        def split_matmul(pe, dst, l_hi, l_lo, m_hi, m_lo, start, stop):
            pe.matmul(dst, l_hi, m_hi, start=start, stop=False)
            pe.matmul(dst, l_hi, m_lo, start=False, stop=False)
            return pe.matmul(dst, l_lo, m_hi, start=False, stop=stop)

        def att3(j):
            return att[j][:, :].rearrange("p (b c) -> p b c", c=W)

        def sc4(j):
            return sc[:, j * B * P:(j + 1) * B * P].rearrange("p (t s h) -> p t s h", s=B, h=H)

        def slot_of(ring, k):
            return ring[:, (k % 2) * B * P:(k % 2 + 1) * B * P]

        LAST = B - 1
        EARLY = [(i % JT, i // JT) for i in range(JT * LAST)]
        EARLY_DVE = 4
        EARLY_SLOT = [7, 8, 8, 9, 10, 11, 12, 12, 13, 14, 15, 16, 16, 17]
        POOL_VALUES = [[3], [1, 3], [1, 3], [1, 3]]
        DVE_SUMS = [EARLY_DVE + 2 + sum(GT - len(x) for x in POOL_VALUES[:g + 1]) for g in range(GROUPS)]
        BETWEEN = {(0, 3): [("h", 1)], (0, 5): [("onehot", 1)], (0, 7): [("values", 2)],
                   (1, 3): [("h", 2)], (1, 5): [("onehot", 2)], (1, 7): [("values", 3)],
                   (2, 3): [("h", 3)], (2, 5): [("onehot", 3)]}

        HIGH_DVE = (13, 14)

        def row_products(eng, slot, j, t, keys, done):
            eng.tensor_tensor(slot[:, 0:keys * P].rearrange("p (s c) -> p s c", c=P), att3(j)[:, 0:keys, P:2 * P],
                              att3(j)[:, t, 0:P].unsqueeze(1).broadcast_to((P, keys, P)), ALU.mult).then_inc(done, 1)

        def column_products(eng, slot, j, done):
            eng.tensor_tensor(slot[:, 0:LAST * P].rearrange("p (t c) -> p t c", c=P), att3(j)[:, 0:LAST, 0:P],
                              att3(j)[:, LAST, P:2 * P].unsqueeze(1).broadcast_to((P, LAST, P)),
                              ALU.mult).then_inc(done, 1)

        def value_products(eng, slot, g, i, done):
            j, t = g // 2, GT * (g % 2) + i
            eng.tensor_tensor(slot.rearrange("p (s h d) -> p s h d", h=H, d=DH),
                              att3(j)[:, :, 2 * P:3 * P].rearrange("p s (h d) -> p s h d", d=DH),
                              sc4(j)[:, t].unsqueeze(3).broadcast_to((P, B, H, DH)), ALU.mult).then_inc(done, 1)

        @block.sync
        def _(sp):
            sp.dma_start(x_sb[:, 0:T], xT[:, 0:T]).then_inc(ld_x0, 16)

            def load_expert(e):
                if e >= 2:
                    sp.wait_ge(w_lo_done, e - 1)
                    sp.wait_ge(wd_lo_pool, e - 1)
                at = (e % 2) * 3 * F
                sp.dma_start(w_raw[:, at:at + 3 * F], experts[e]).then_inc(ld_w[e], 16)

            load_expert(0)
            sp.dma_start(fs_bc[:, :], fside.broadcast_to((P, B * E))).then_inc(ld_small, 16)
            sp.dma_start(pr_bc[:, :], prob.broadcast_to((P, B))).then_inc(ld_small, 16)
            sp.dma_start(it_bc[:, :], itok.broadcast_to((P, B))).then_inc(ld_small, 16)
            sp.dma_start(col[:, :], cols).then_inc(ld_small, 16)
            sp.dma_start(const[:, :], consts).then_inc(ld_small, 16)
            sp.dma_start(small_sb[0:A, :], small).then_inc(ld_small, 16)
            load_expert(1)
            sp.dma_start(x_sb[:, T:B * T], xT[:, T:B * T]).then_inc(ld_x, 16)
            sp.dma_start(x_sb[:, B * T:(B + 1) * T], xT[:, 0:T]).then_inc(ld_x, 16)
            sp.dma_start(projw[:, :], proj).then_inc(ld_proj, 16)
            load_expert(2)
            sp.dma_start(masks_sb[:, :].bitcast(U16), masks).then_inc(ld_masks, 16)
            sp.dma_start(spread_raw[:, :], spread).then_inc(ld_spread, 16)
            load_expert(3)
            sp.dma_start(gather_c[:, :], gather).then_inc(ld_const, 16)
            sp.dma_start(ident[:, :], ident_in).then_inc(ld_const, 16)
            sp.dma_start(row_bc[:, :], rows.broadcast_to((P, R_END))).then_inc(ld_const, 16)
            for e in range(4, NE):
                load_expert(e)

            def store_batch(pb):
                row = slice(pb, pb + 1)
                sp.wait_ge(x2n_done, pb + 1)
                sp.dma_start(x2_dram[:, row, :], x2n[:, :].unsqueeze(1)).then_inc(x2n_sent, 16)
                sp.wait_ge(pooled_done, 2 * pb + 2)
                sp.wait_ge(qkv_done, 2 * pb + 2)
                sp.dma_start(qkvp_dram[:, row, :, :],
                             stage[:, :].rearrange("p (j c) -> p j c", j=JT).unsqueeze(1)).then_inc(qkv_sent, 16)
                sp.wait_ge(qkv_sent, 16 * pb + 16)

            for pb in range(B - 1):
                store_batch(pb)
            sp.wait_ge(down_done, B * UNITS)
            for j in range(JT):
                sp.dma_start(att[j][:, 0:LAST * W].rearrange("p (b c) -> p b c", c=W),
                             qkvp_dram[:, 0:LAST, j, :]).then_inc(ld_att[j], 16)
            sp.dma_start(w1_raw[:, :], moe_w1).then_inc(ld_f, 16)
            sp.dma_start(w2_sb[:, :], moe_w2).then_inc(ld_f, 16)
            sp.dma_start(b2_sb[0:E, :], moe_b2).then_inc(ld_f, 16)
            sp.dma_start(big_b[0:E, :].bitcast(U16), big).then_inc(ld_f, 16)
            sp.dma_start(x2_all[:, 0:LAST * T].rearrange("p (b c) -> p b c", c=T),
                         x2_dram[:, 0:LAST, :]).then_inc(ld_x2, 16)
            for g in range(GROUPS):
                j, b0 = g // 2, GT * (g % 2)
                sp.wait_ge(fin_done, g + 1)
                sp.dma_start(out[b0:b0 + GT, j * P:(j + 1) * P, :].rearrange("b p c -> p b c"),
                             zf[:, (g % 2) * GC:(g % 2 + 1) * GC].rearrange("p (b c) -> p b c", c=P))\
                    .then_inc(out_sent[g % 2], 16)
            for i in range(2):
                sp.wait_ge(out_sent[i], 16 * GROUPS // 2)

        @block.gpsimd
        def _(pool):
            nc.gpsimd.memset(ones[:, :], 1.0).then_inc(setup_step, 1)
            nc.gpsimd.memset(mean_col[:, :], 1.0 / P).then_inc(setup_step, 1)
            for e in range(NE):
                for kind, hi_ready, done in ((1, w_hi_done, w_lo_pool), (2, wd_hi_done, wd_lo_pool)):
                    pool.wait_ge(hi_ready, e + 1)
                    a, s = (e * 3 + kind) * F, (e % 2 * 3 + kind) * F
                    nc.gpsimd.tensor_tensor(w_lo[:, a:a + F], w_raw[:, s:s + F],
                                            w_hi[:, a:a + F].bitcast(F32), ALU.subtract).then_inc(done, 1)

            def query_states(pb):
                pool.wait_ge(q_done, pb + 1)
                for m in range(4):
                    pool.wait_ge(state_done, 4 * pb + m + 1)
                    s = state[:, m * 512:m * 512 + 512].rearrange("p (a t) -> p a t", a=2)
                    nc.gpsimd.tensor_tensor(s, s, qT[:, :].unsqueeze(1).broadcast_to((P, 2, T)),
                                            ALU.mult).then_inc(qs_done, 1)

            def scale_norm(pb):
                pool.wait_ge(cen_done, pb + 1)
                pool.wait_ge(gammaT_done, pb + 1)
                nc.gpsimd.tensor_tensor(scaledT[:, :], cenT[:, :], gammaT[:, :], ALU.mult).then_inc(scaled_done, 1)

            def mask_of(pb):
                step = mask_step_of(pb)
                for k, kind in enumerate((sel_u, sel_l, sel_d)):
                    part = mask_now if k == 0 else mask_part
                    step(nc.gpsimd.tensor_tensor(part[:, :], masks_sb[:, k * JT * T:(k + 1) * JT * T],
                                                 kind[:, bass.ds(pb, 1)].broadcast_to((P, JT * T)), ALU.mult))
                    if k == 1:
                        step(nc.gpsimd.tensor_tensor(mask_now[:, :], mask_now[:, :], mask_part[:, :], ALU.add))
                nc.gpsimd.tensor_tensor(mask_now[:, :], mask_now[:, :], mask_part[:, :],
                                        ALU.add).then_inc(mask_now_done, 1)

            def mask_step_of(pb):
                k = [0]

                def step(ins):
                    k[0] += 1
                    ins.then_inc(mask_step, 1)
                    pool.wait_ge(mask_step, pb * 4 + k[0])
                return step

            pool.wait_ge(ld_masks, 16)
            pool.wait_ge(kinds_done, 1)
            with pool.Fori(0, B) as pb:
                query_states(pb)
                scale_norm(pb)
                mask_of(pb)

            for j in range(JT):
                pool.wait_ge(ld_att[j], 16)
            used = 0

            def free_slot():
                if used >= 2:
                    pool.wait_ge(read_pool, used - 1)
                return slot_of(ring_pool, used)

            for j, t in EARLY[EARLY_DVE:]:
                row_products(nc.gpsimd, free_slot(), j, t, LAST, prod_pool)
                used += 1
            pool.wait_ge(x2n_done, B)
            nc.gpsimd.tensor_copy(x2_all[:, LAST * T:B * T], x2n[:, :]).then_inc(x2_kept, 1)
            pool.wait_ge(qkv_done, JT * B)
            row_products(nc.gpsimd, free_slot(), 1, LAST, B, prod_pool)
            used += 1
            column_products(nc.gpsimd, free_slot(), 1, prod_pool)
            used += 1
            pool.wait_ge(pooled_done, JT * B)
            summed = 0
            for g in range(GROUPS):
                j, b0 = g // 2, GT * (g % 2)
                nc.gpsimd.tensor_tensor(resid[:, g * GC:(g + 1) * GC].rearrange("p (b c) -> p b c", c=P),
                                        att3(j)[:, b0:b0 + GT, QKV:W],
                                        row_bc[:, R_OUTB:R_OUTB + P].unsqueeze(1).broadcast_to((P, GT, P)),
                                        ALU.add).then_inc(resid_done, 1)
                pool.wait_ge(p_done, g + 1)
                if g == 0:
                    pool.wait_ge(read_pool, used)
                if g >= 2:
                    pool.wait_ge(atT_ready, g - 1)
                for i in POOL_VALUES[g]:
                    slot = slot_of(ring_pool, used)
                    used += 1
                    value_products(nc.gpsimd, slot, g, i, tree_pool)
                    for k, half in enumerate((4 * P, 2 * P, P)):
                        pool.wait_ge(tree_pool, 3 * summed + k + 1)
                        dst = slot[:, 0:half] if half > P else atn[:, (g % 2) * GC + i * P:(g % 2) * GC + (i + 1) * P]
                        ins = nc.gpsimd.tensor_tensor(dst, slot[:, 0:half], slot[:, half:2 * half], ALU.add)
                        ins.then_inc(tree_pool if half > P else sum_pool, 1)
                    summed += 1

        @block.scalar
        def _(act):
            def split_weights(e):
                act.wait_ge(ld_w[e], 16)
                s = (e % 2) * 3 * F
                nc.scalar.activation(w_hi[:, e * 3 * F:(e * 3 + 2) * F], w_raw[:, s:s + 2 * F],
                                     ACT.Copy).then_inc(w_hi_done, 1)

            def split_x(b):
                nc.scalar.activation(x_hi[:, bass.ds(b % 2 * T, T)], x_sb[:, bass.ds(b * T, T)],
                                     ACT.Copy).then_inc(x_hi_done, 1)

            def h_high(done, m):
                act.wait_ge(h_done, done + m + 1)
                if not (isinstance(done, int) and done + m < 2):
                    act.wait_ge(down_done, done + m - 1)
                s = (m % 2) * 2 * T
                nc.scalar.activation(h_hi[:, s:s + 2 * T], hidden[:, s:s + 2 * T], ACT.Copy).then_inc(hi_done, 1)

            def exponentials(pb):
                for j in range(JT):
                    act.wait_ge(masked, JT * pb + j + 1)
                    nc.scalar.activation(ex[:, j * T:(j + 1) * T], mk[:, j * T:(j + 1) * T], ACT.Exp,
                                         bias=mxn[:, j:j + 1], scale=-1.0,
                                         accum_out=ssum[:, j:j + 1]).then_inc(exp_done, 1)

            def chain(n, b, pb, last):
                if n == 2:
                    act.wait_ge(down_done, b * UNITS)
                    nc.scalar.activation(c_hi[:, :], acc[:, 0:T], ACT.Copy).then_inc(cond_hi, 1)
                if n == 3:
                    act.wait_ge(kvqg_ready, b)
                    nc.scalar.activation(v_hi[:, :], r0[:, T:2 * T], ACT.Copy).then_inc(v_hi_done, 1)
                    nc.scalar.activation(kT[:, :], r0[:, 0:T], ACT.Copy).then_inc(k_done, 1)
                if n == 4:
                    nc.scalar.activation(qT[:, :], r1[:, 0:T], ACT.Copy, scale=HEAD_SCALE).then_inc(q_done, 1)
                    nc.scalar.activation(gT[:, :], r1[:, T:2 * T], ACT.Silu,
                                         bias=col[:, C_BG:C_BG + 1]).then_inc(gate_done, 1)
                if n == 5:
                    act.wait_ge(gate_done, b)
                    nc.scalar.activation(gammaT[:, :], gT[:, :], ACT.Copy,
                                         scale=col[:, C_GAMMA:C_GAMMA + 1]).then_inc(gammaT_done, 1)
                    nc.scalar.activation(betaT[:, :], gT[:, :], ACT.Copy,
                                         scale=col[:, C_BETA:C_BETA + 1]).then_inc(betaT_done, 1)
                if n == 8:
                    act.wait_ge(cen_ready, b)
                    nc.scalar.activation(cenT[:, :], r1[:, 0:T], ACT.Copy).then_inc(cen_done, 1)
                    nc.scalar.activation(sqT[:, :], r1[:, 0:T], ACT.Square).then_inc(sq_done, 1)
                if n == 13:
                    act.wait_ge(pre_ready, b)
                    nc.scalar.activation(atT[0:A, :], r2[0:A, 0:T], ACT.Tanh,
                                         bias=small_sb[0:A, 0:1]).then_inc(at_done, 1)
                    act.wait_ge(x2t_ready, b)
                    nc.scalar.activation(x2n[:, :], r1[:, 0:T], ACT.Copy).then_inc(x2n_done, 1)
                if n == 17:
                    act.wait_ge(pooled_ready, b)
                    nc.scalar.activation(plT[:, :], r0[:, 0:T], ACT.Copy).then_inc(plT_done, 1)
                if n == 17 and not last:
                    act.wait_ge(x2n_sent, 16 * b)

            def batch(b, first=False, last=False):
                for n in range(UNITS):
                    if not first:
                        chain(n, b, b - 1, last)
                    ahead = not first and n == 9
                    if ahead and not last:
                        h_high(b * UNITS, n - 1)
                    if not last:
                        act.wait_ge(g_ready, b * UNITS + n + 1)
                        if n >= 2 or not first:
                            act.wait_ge(lo_done, b * UNITS + n - 1)
                        s = (n % 2) * 2 * T
                        nc.scalar.activation(hidden[:, s:s + 2 * T], pg[n % 2][:, :], ACT.Silu).then_inc(silu_done, 1)
                        if n == 12:
                            if first:
                                act.wait_ge(ld_x, 32)
                            split_x(b + 1)
                    if n == 14 and not first:
                        exponentials(b - 1)
                    if n >= 1 and not last and not ahead and (first or n - 1 not in HIGH_DVE):
                        h_high(b * UNITS, n - 1)
                    if n == 0 and not first:
                        h_high((b - 1) * UNITS, UNITS - 1)
                    if first:
                        if n % 2 == 0 and n // 2 + 1 < NE:
                            split_weights(n // 2 + 1)
                        if n == 5:
                            act.wait_ge(ld_proj, 16)
                            nc.scalar.activation(p_hi[:, :], projw[:, 0:4 * P], ACT.Copy).then_inc(p_hi_done, 1)
                        if n == 11:
                            act.wait_ge(ld_spread, 16)
                            nc.scalar.activation(spread_r[:, :], spread_raw[:, :], ACT.Copy).then_inc(spread_done, 1)

            act.wait_ge(ld_x0, 16)
            split_x(0)
            split_weights(0)
            batch(0, first=True)
            with act.Fori(1, B) as b:
                batch(b)
            batch(B, last=True)

            def softmax_exp(g):
                j, a = g // 2, g * GC
                act.wait_ge(soft_step, 2 * g + 2)
                nc.scalar.activation(sc[:, a:a + GC], sc[:, a:a + GC], ACT.Exp, scale=HEAD_SCALE).then_inc(fexp_done, 1)

            def values_copy(g):
                act.wait_ge(atT_ready, g + 1)
                nc.scalar.activation(ctxT[:, (g % 2) * GC:(g % 2 + 1) * GC], pg[0][:, :], ACT.Copy).then_inc(ctx_done, 1)

            def h_copy(g):
                act.wait_ge(hT_ready, g + 1)
                if g >= 2:
                    act.wait_ge(fpre_ready, E * (g - 1))
                nc.scalar.activation(hT_hi[:, (g % 2) * GC:(g % 2 + 1) * GC], r1[:, :], ACT.Copy)\
                    .then_inc(hT_hi_done, 1)
                nc.scalar.activation(hT[:, (g % 2) * GC:(g % 2 + 1) * GC], r1[:, :], ACT.Copy).then_inc(hT_done, 1)

            def onehot_copy(g):
                act.wait_ge(ohT_ready, g + 1)
                c = slice((g % 2) * GC, (g % 2 + 1) * GC)
                nc.scalar.activation(ohT_b[0:E, c], r2[0:E, :], ACT.Copy).then_inc(ohT_done, 1)
                nc.scalar.activation(ohT[0:E, c], r2[0:E, :], ACT.Copy).then_inc(ohT_done, 1)

            def expert_gelu(g, e):
                n = g * E + e
                act.wait_ge(fpre_ready, n + 1)
                if n >= 2:
                    act.wait_ge(he_used, n - 1)
                nc.scalar.activation(he[:, (n % 2) * GC:(n % 2 + 1) * GC], pu[n % 2][:, :], ACT.Gelu,
                                     bias=col[:, C_B1 + e:C_B1 + e + 1]).then_inc(gelu_done, 1)

            act.wait_ge(ld_f, 64)
            nc.scalar.activation(w1_hi[:, :], w1_raw[:, :], ACT.Copy).then_inc(w1_hi_done, 1)
            softmax_exp(0)
            softmax_exp(1)
            values_copy(0)
            softmax_exp(2)
            values_copy(1)
            h_copy(0)
            softmax_exp(3)
            onehot_copy(0)
            for g in range(GROUPS):
                for e in range(E):
                    expert_gelu(g, e)
                    for what, to in BETWEEN.get((g, e), ()):
                        {"values": values_copy, "h": h_copy, "onehot": onehot_copy}[what](to)

        @block.vector
        def _(dve):
            vec = nc.vector

            dve.wait_ge(ld_small, 96)
            count = [0]

            def step(ins):
                count[0] += 1
                ins.then_inc(setup_dve_step, 1)
                dve.wait_ge(setup_dve_step, count[0])

            co = coef[:, :].rearrange("p (b e) -> p b e", e=NE)
            step(vec.tensor_scalar(itf[:, :], pr_bc[:, :], -1.0, 1.0, ALU.mult, ALU.add))
            step(vec.tensor_tensor(co[:, :, 0:E], fs_bc[:, :].rearrange("p (b e) -> p b e", e=E),
                                   itf[:, :].unsqueeze(2).broadcast_to((P, B, E)), ALU.mult))
            step(vec.tensor_copy(co[:, :, E:NE], pr_bc[:, :].unsqueeze(2)))

            def split_x(b):
                dve.wait_ge(x_hi_done, b + 1)
                vec.tensor_tensor(x_lo[:, bass.ds(b % 2 * T, T)], x_sb[:, bass.ds(b * T, T)],
                                  x_hi[:, bass.ds(b % 2 * T, T)].bitcast(F32), ALU.subtract).then_inc(x_lo_done, 1)

            def split_weights(e):
                dve.wait_ge(w_hi_done, e + 1)
                a, s = e * 3 * F, (e % 2) * 3 * F
                vec.tensor_tensor(w_lo[:, a:a + F], w_raw[:, s:s + F],
                                  w_hi[:, a:a + F].bitcast(F32), ALU.subtract).then_inc(w_lo_done, 1)
                a, s = a + 2 * F, s + 2 * F
                vec.tensor_copy(w_hi[:, a:a + F], w_raw[:, s:s + F]).then_inc(wd_hi_done, 1)

            def setup(n):
                if n == 13:
                    step(vec.tensor_copy(itf[:, :], it_bc[:, :]))
                    step(vec.tensor_scalar(sel_u[:, :], itf[:, :], 0.0, None, ALU.is_equal))
                    step(vec.tensor_scalar(sel_l[:, :], itf[:, :], 1.0, None, ALU.is_equal))
                    step(vec.tensor_tensor(sel_d[:, :], sel_u[:, :], sel_l[:, :], ALU.add))
                if n == 14:
                    step(vec.tensor_scalar(sel_d[:, :], sel_d[:, :], -1.0, 1.0, ALU.mult, ALU.add))
                    vec.tensor_copy(itf[:, :], sel_d[:, :]).then_inc(kinds_done, 1)
                if n in (15, 16):
                    j = n - 15
                    c = cnt[:, :].rearrange("p (b j) -> p b j", j=JT)[:, :, j]
                    k = K_CNT + 3 * j
                    step(vec.tensor_scalar(c, sel_u[:, :], const[:, k:k + 1], None, ALU.mult))
                    step(vec.scalar_tensor_tensor(out=c, in0=sel_l[:, :], scalar=const[:, k + 1:k + 2], in1=c,
                                                  op0=ALU.mult, op1=ALU.add))
                    step(vec.scalar_tensor_tensor(out=c, in0=sel_d[:, :], scalar=const[:, k + 2:k + 3], in1=c,
                                                  op0=ALU.mult, op1=ALU.add))
                if n == 17:
                    step(vec.tensor_scalar(nv_rep[0:A, :], ones[0:A, :], small_sb[0:A, 1:2], -1.0,
                                           ALU.mult, ALU.mult))
                if n == 5:
                    dve.wait_ge(p_hi_done, 1)
                    vec.tensor_tensor(p_lo[:, :], projw[:, 0:4 * P], p_hi[:, :].bitcast(F32),
                                      ALU.subtract).then_inc(p_lo_done, 1)

            def h_low(done, m):
                dve.wait_ge(hi_done, done + m + 1)
                s = (m % 2) * 2 * T
                vec.tensor_tensor(h_lo[:, s:s + 2 * T], hidden[:, s:s + 2 * T], h_hi[:, s:s + 2 * T].bitcast(F32),
                                  ALU.subtract).then_inc(lo_done, 1)

            def h_high(done, m):
                dve.wait_ge(h_done, done + m + 1)
                dve.wait_ge(down_done, done + m - 1)
                s = (m % 2) * 2 * T
                vec.tensor_copy(h_hi[:, s:s + 2 * T], hidden[:, s:s + 2 * T]).then_inc(hi_done, 1)

            def hidden_values(b, n):
                dve.wait_ge(silu_done, b * UNITS + n + 1)
                dve.wait_ge(u_ready, b * UNITS + n + 1)
                s = (n % 2) * 2 * T
                vec.scalar_tensor_tensor(out=hidden[:, s:s + 2 * T], in0=hidden[:, s:s + 2 * T],
                                         scalar=coef[:, bass.ds(b * NE + n // 2, 1)], in1=pu[n % 2][:, :],
                                         op0=ALU.mult, op1=ALU.mult).then_inc(h_done, 1)

            def guess(steps, src, eps, w, wi, n):
                v = w[:, 0:n]
                steps(vec.tensor_scalar(v, src, eps, None, ALU.add))
                steps(vec.tensor_scalar(wi[:, 0:n], v.bitcast(I32), 1, None, ALU.logical_shift_right))
                steps(vec.tensor_scalar(wi[:, n:2 * n], wi[:, 0:n], -1.0, MAGIC, ALU.mult, ALU.add))
                return wi[:, n:2 * n].bitcast(F32)

            def newton(steps, g_in, w, n, times):
                v, g, a = w[:, 0:n], w[:, n:2 * n], w[:, 2 * n:3 * n]
                for _ in range(times):
                    steps(vec.scalar_tensor_tensor(out=a, in0=g_in, scalar=-0.5, in1=g_in, op0=ALU.mult, op1=ALU.mult))
                    steps(vec.tensor_tensor(a, a, v, ALU.mult))
                    steps(vec.scalar_tensor_tensor(out=g, in0=a, scalar=1.5, in1=g_in, op0=ALU.add, op1=ALU.mult))
                    g_in = g
                return g

            def rsqrt(steps, src, eps, w, wi, n):
                return newton(steps, guess(steps, src, eps, w, wi, n), w, n, NEWTON)

            def stepper(semaphore, base):
                k = [0]

                def run(ins):
                    k[0] += 1
                    ins.then_inc(semaphore, 1)
                    dve.wait_ge(semaphore, base + k[0])
                return run

            def scan(m):
                s = (m % 2) * 2 * T
                vec.tensor_tensor_scan(state[:, m * 512:m * 512 + 512], const[:, K_DECAY:K_DECAY + 512],
                                       kv[:, s:s + 512], 0.0, ALU.mult, ALU.add).then_inc(state_done, 1)

            def outer(pb, m):
                dve.wait_ge(vb_ready, 4 * pb + m + 1)
                s = (m % 2) * 2 * T
                src = (r2, r0)[m % 2]
                vec.tensor_tensor(kv[:, s:s + 512].rearrange("p (a t) -> p a t", a=2),
                                  src[:, :].rearrange("p (a t) -> p a t", a=2),
                                  kT[:, :].unsqueeze(1).broadcast_to((P, 2, T)), ALU.mult).then_inc(kv_done, 1)

            def gated_norm(b, pb):
                dve.wait_ge(bc_ready, b)
                dve.wait_ge(scaled_done, b)
                dve.wait_ge(betaT_done, b)
                st = stepper(ln_step, pb * 2)
                st(vec.tensor_tensor(lnT[:, :], scaledT[:, :], r2[:, T:2 * T], ALU.mult))
                st(vec.tensor_tensor(lnT[:, :], lnT[:, :], betaT[:, :], ALU.add))

            def rstd_begin(b, pb):
                dve.wait_ge(var_ready, b)
                st = stepper(rstd_step, pb * (RSTEPS + JT))
                newton(st, guess(st, r2[:, 0:JT], RET_EPS, nw, nwi, JT), nw, JT, 1)

            def rstd_end(pb):
                g = newton(stepper(rstd_step, pb * (RSTEPS + JT) + 6), nw[:, JT:2 * JT], nw, JT, NEWTON - 1)
                for j in range(JT):
                    vec.tensor_scalar(diag[:, j * P:(j + 1) * P], ident[:, :], g[:, j:j + 1], None,
                                      ALU.mult).then_inc(rstd_step, 1)

            def chain(n, b, pb, last):
                if n == 2:
                    dve.wait_ge(cond_hi, b)
                    vec.tensor_tensor(c_lo[:, :], acc[:, 0:T], c_hi[:, :].bitcast(F32),
                                      ALU.subtract).then_inc(cond_lo, 1)
                if n == 3:
                    dve.wait_ge(v_hi_done, b)
                    dve.wait_ge(k_done, b)
                    vec.tensor_tensor(v_lo[:, :], r0[:, T:2 * T], v_hi[:, :].bitcast(F32),
                                      ALU.subtract).then_inc(v_lo_done, 1)
                if n == 4:
                    outer(pb, 0)
                    outer(pb, 1)
                    dve.wait_ge(kv_done, 4 * pb + 1)
                    scan(0)
                if n == 5:
                    dve.wait_ge(state_done, 4 * pb + 1)
                    outer(pb, 2)
                    dve.wait_ge(kv_done, 4 * pb + 2)
                    scan(1)
                    dve.wait_ge(kv_done, 4 * pb + 3)
                    scan(2)
                if n == 6:
                    dve.wait_ge(state_done, 4 * pb + 2)
                    outer(pb, 3)
                    dve.wait_ge(kv_done, 4 * pb + 4)
                    scan(3)
                if n == 12:
                    dve.wait_ge(wo_ready, b)
                    vec.scalar_tensor_tensor(out=x2T[:, :], in0=r0[:, 0:T], scalar=col[:, C_BO:C_BO + 1],
                                             in1=x_sb[:, bass.ds(pb * T, T)], op0=ALU.add,
                                             op1=ALU.add).then_inc(x2_done, 1)
                if n == 14:
                    dve.wait_ge(s_ready, b)
                    dve.wait_ge(mask_now_done, b)
                    vec.tensor_scalar(cnt_now[:, :], cnt[:, bass.ds(pb * JT, JT)], 1.0, None,
                                      ALU.mult).then_inc(cnt_done, 1)
                    for j in range(JT):
                        vec.tensor_tensor_reduce(mk[:, j * T:(j + 1) * T], r0[:, 0:T],
                                                 mask_now[:, j * T:(j + 1) * T], 1.0, 3e38,
                                                 ALU.add, ALU.min, mxn[:, j:j + 1]).then_inc(masked, 1)
                if n == 17:
                    dve.wait_ge(cnt_done, b)
                    dve.wait_ge(exp_done, JT * pb + JT)
                    st = stepper(rn_step, pb * 2)
                    st(vec.tensor_tensor(rn[:, 0:JT], ssum[:, :], cnt_now[:, :], ALU.mult))
                    st(vec.reciprocal(rn[:, JT:2 * JT], rn[:, 0:JT]))
                    dve.wait_ge(pooled_ready, b)
                    if not last:
                        dve.wait_ge(x2n_sent, 16 * b)
                    for j in range(JT):
                        dst = att[j][:, LAST * W:B * W] if last else stage[:, j * W:(j + 1) * W]
                        vec.tensor_scalar(dst[:, QKV:W], r2[:, j * P:(j + 1) * P], rn[:, JT + j:JT + j + 1],
                                          None, ALU.mult).then_inc(pooled_done, 1)
                if n == UNITS:
                    for j in range(JT):
                        dve.wait_ge(qkv_ready, JT * pb + j + 1)
                        dst = att[j][:, LAST * W:B * W] if last else stage[:, j * W:(j + 1) * W]
                        vec.scalar_tensor_tensor(out=dst[:, 0:QKV], in0=(r1, r2)[j][:, 0:QKV],
                                                 scalar=rn[:, JT + j:JT + j + 1], in1=row_bc[:, R_INB:R_INB + QKV],
                                                 op0=ALU.mult, op1=ALU.add).then_inc(qkv_done, 1)

            made = [0]
            taken = [0]

            def free_slot():
                if made[0] >= 2:
                    dve.wait_ge(sum_dve, made[0] - 1)
                return slot_of(ring_dve, made[0])

            def sum_own(dst, width, **kw):
                made[0] += 1
                dve.wait_ge(prod_dve, made[0])
                vec.tensor_reduce(dst, width(slot_of(ring_dve, made[0] - 1)), AX.X, ALU.add).then_inc(sum_dve, 1)

            def sum_pooled(dst, width):
                taken[0] += 1
                dve.wait_ge(prod_pool, taken[0])
                vec.tensor_reduce(dst, width(slot_of(ring_pool, taken[0] - 1)), AX.X, ALU.add).then_inc(read_pool, 1)

            def heads(n):
                return lambda slot: slot[:, 0:n * P].rearrange("p (s h d) -> p s h d", h=H, d=DH)

            def early_scores(i):
                j, t = EARLY[i]
                dst = sc4(j)[:, t, 0:LAST, :]
                if i == 0:
                    for k in range(JT):
                        dve.wait_ge(ld_att[k], 16)
                if i < EARLY_DVE:
                    row_products(vec, free_slot(), j, t, LAST, prod_dve)
                    sum_own(dst, heads(LAST))
                else:
                    sum_pooled(dst, heads(LAST))

            def batch(b, first=False, last=False):
                for n in range(UNITS + 1):
                    if not first:
                        chain(n, b, b - 1, last)
                    if last:
                        for i, at in enumerate(EARLY_SLOT):
                            if at == n:
                                early_scores(i)
                    if n == UNITS:
                        break
                    ahead = not first and n in (9, 10, 14, 15)

                    def low_part():
                        if n >= 1 and not last:
                            h_low(b * UNITS, n - 1)
                        if n == 0 and not first:
                            h_low((b - 1) * UNITS, UNITS - 1)

                    if not first and not last and n - 1 in HIGH_DVE:
                        h_high(b * UNITS, n - 1)
                    if ahead and n != 14:
                        low_part()
                    if not first:
                        if n == 9:
                            rstd_begin(b, b - 1)
                        if n == 15:
                            dve.wait_ge(pt_ready, b)
                            vec.tensor_copy(pT[:, :], r1[:, :]).then_inc(pt_done, 1)
                    if not last:
                        hidden_values(b, n)
                        if n == 12:
                            split_x(b + 1)
                    if n == 9 and not first:
                        rstd_end(b - 1)
                    if n == 11 and not first:
                        gated_norm(b, b - 1)
                    if not ahead or n == 14:
                        low_part()
                    if first and n % 2 == 0 and n // 2 + 1 < NE:
                        split_weights(n // 2 + 1)
                    if first:
                        setup(n)

            split_x(0)
            split_weights(0)
            dve.wait_ge(setup_step, 2)
            batch(0, first=True)
            dve.wait_ge(ld_const, 48)
            with dve.Fori(1, B) as b:
                batch(b)
            batch(B, last=True)

            def last_scores():
                dve.wait_ge(qkv_done, JT * B)
                row_products(vec, free_slot(), 0, LAST, B, prod_dve)
                sum_own(sc4(0)[:, LAST], heads(B))
                column_products(vec, free_slot(), 0, prod_dve)
                sum_own(sc4(0)[:, 0:LAST, LAST, :], heads(LAST))

            def last_scores_pooled():
                sum_pooled(sc4(1)[:, LAST], heads(B))
                sum_pooled(sc4(1)[:, 0:LAST, LAST, :], heads(LAST))

            def softmax(g):
                natural = sc4(g // 2)[:, GT * (g % 2):GT * (g % 2) + GT]
                by_head = natural.rearrange("p t s h -> p t h s")
                n = GT * H
                mx = smx[:, g * n:(g + 1) * n].rearrange("p (t h) -> p t h", h=H)
                sm = ssm[:, g * n:(g + 1) * n].rearrange("p (t h) -> p t h", h=H)
                st = stepper(soft_step, 2 * g)
                dve.wait_ge(sum_dve, made[0])
                dve.wait_ge(read_pool, taken[0])
                st(vec.tensor_reduce(mx, by_head, AX.X, ALU.max))
                st(vec.tensor_tensor(natural, natural, mx.unsqueeze(2).broadcast_to((P, GT, B, H)), ALU.subtract))
                return natural, by_head, mx, sm

            def softmax_norm(g, natural, by_head, mx, sm):
                st = stepper(norm_step, 2 * g)
                dve.wait_ge(fexp_done, g + 1)
                st(vec.tensor_reduce(sm, by_head, AX.X, ALU.add))
                st(vec.reciprocal(mx, sm))
                vec.tensor_tensor(natural, natural, mx.unsqueeze(2).broadcast_to((P, GT, B, H)),
                                  ALU.mult).then_inc(p_done, 1)

            def values(g):
                dve.wait_ge(p_done, g + 1)
                if g >= 2:
                    dve.wait_ge(atT_ready, g - 1)
                for i in range(GT):
                    if i not in POOL_VALUES[g]:
                        value_products(vec, free_slot(), g, i, prod_dve)
                        at = (g % 2) * GC + i * P
                        sum_own(atn[:, at:at + P], lambda slot: slot.rearrange("p (s c) -> p c s", c=P))

            norm_steps = [0]

            def norm(src, last_use, g_row, b_row, done, before):
                if last_use:
                    dve.wait_ge(*last_use)
                base = norm_steps[0]
                for t in range(GT):
                    vec.bn_stats(stats[:, t * 6:t * 6 + 6], src[:, t * P:(t + 1) * P]).then_inc(stat_step, 1)
                for t in range(GT):
                    dve.wait_ge(stat_step, base + t + 1)
                    vec.bn_aggr(aggr[:, 2 * t:2 * t + 2], stats[:, t * 6:t * 6 + 6]).then_inc(stat_step, 1)
                base += 2 * GT
                dve.wait_ge(stat_step, base)
                var = aggr[:, :].rearrange("p (t k) -> p t k", k=2)[:, :, 1]
                r = rsqrt(stepper(stat_step, base), var, LN_EPS, nf, nfi, GT)
                norm_steps[0] = base + RSTEPS
                for t in range(GT):
                    c = slice(t * P, t * P + P)
                    vec.scalar_tensor_tensor(out=src[:, c], in0=src[:, c], scalar=aggr[:, 2 * t:2 * t + 1],
                                             in1=row_bc[:, g_row:g_row + P], op0=ALU.subtract,
                                             op1=ALU.mult).then_inc(done, 1)
                for t in range(GT):
                    c = slice(t * P, t * P + P)
                    dve.wait_ge(done, before + t + 1)
                    vec.scalar_tensor_tensor(out=src[:, c], in0=src[:, c], scalar=r[:, t:t + 1],
                                             in1=row_bc[:, b_row:b_row + P], op0=ALU.mult,
                                             op1=ALU.add).then_inc(done, 1)
                return done, before + 2 * GT

            used = [None]

            def attention_out(g):
                h = hn[:, g * GC:(g + 1) * GC]
                dve.wait_ge(proj_ready, g + 1)
                dve.wait_ge(resid_done, g + 1)
                vec.tensor_tensor(h, pg[1][:, :], resid[:, g * GC:(g + 1) * GC], ALU.add).then_inc(y_done, 1)
                dve.wait_ge(y_done, g + 1)
                used[0] = norm(h, used[0], R_G1, R_B1, h_step, 2 * GT * g)

            def h_low_part(g):
                dve.wait_ge(hT_hi_done, g + 1)
                dve.wait_ge(hT_done, g + 1)
                c = slice((g % 2) * GC, (g % 2 + 1) * GC)
                vec.tensor_tensor(hT_lo[:, c], hT[:, c], hT_hi[:, c].bitcast(F32), ALU.subtract).then_inc(hT_lo_done, 1)

            def route(g):
                dve.wait_ge(logit_ready, g + 1)
                st = stepper(route_step, 7 * g)
                l3 = logit[:, :].rearrange("p (t e) -> p t e", e=E)
                st(vec.tensor_tensor(l3, r2[:, 0:GT * E].rearrange("p (t e) -> p t e", e=E),
                                     row_bc[:, R_RB:R_RB + E].unsqueeze(1).broadcast_to((P, GT, E)), ALU.add))
                other = l3.unsqueeze(2).broadcast_to((P, GT, E, E))
                own = l3.unsqueeze(3).broadcast_to((P, GT, E, E))
                gt4 = r_gt[:, :].rearrange("p (t e f) -> p t e f", e=E, f=E)
                eq4 = r_eq[:, :].rearrange("p (t e f) -> p t e f", e=E, f=E)
                eq3 = r_eq[:, :].rearrange("p (t x) -> p t x", t=GT)
                vec.tensor_tensor(gt4, other, own, ALU.is_gt).then_inc(route_gt, 1)
                st(vec.tensor_tensor(eq4, other, own, ALU.is_equal))
                st(vec.tensor_tensor(eq3, eq3, const[:, K_TRI:K_TRI + E * E].unsqueeze(1).broadcast_to((P, GT, E * E)),
                                     ALU.mult))
                dve.wait_ge(route_gt, g + 1)
                st(vec.tensor_tensor(r_gt[:, :], r_gt[:, :], r_eq[:, :], ALU.add))
                st(vec.tensor_reduce(r_rank[:, :], r_gt[:, :].rearrange("p (a f) -> p a f", f=E), AX.X, ALU.add))
                v3 = r_val[:, :].rearrange("p (t e) -> p t e", e=E)
                st(vec.scalar_tensor_tensor(out=v3, in0=r_rank[:, :].rearrange("p (t e) -> p t e", e=E), scalar=2.0,
                                            in1=const[:, K_IDX:K_IDX + E].unsqueeze(1).broadcast_to((P, GT, E)),
                                            op0=ALU.is_lt, op1=ALU.mult))
                st(vec.tensor_reduce(r_max[:, :], v3, AX.X, ALU.max))
                if g >= 1:
                    dve.wait_ge(ohT_ready, g)
                vec.tensor_tensor(onehot[:, :].rearrange("p (t e) -> p t e", e=E), v3,
                                  r_max[:, :].unsqueeze(2).broadcast_to((P, GT, E)),
                                  ALU.is_equal).then_inc(onehot_done, 1)
                dve.wait_ge(onehot_done, g + 1)

            def finish(g):
                z = zf[:, (g % 2) * GC:(g % 2 + 1) * GC]
                dve.wait_ge(he_used, E * (g + 1))
                if g >= 2:
                    dve.wait_ge(out_sent[g % 2], 16)
                vec.tensor_tensor(z, (acc, r0)[g % 2][:, :], hn[:, g * GC:(g + 1) * GC], ALU.add).then_inc(z_done, 1)
                dve.wait_ge(z_done, g + 1)
                used[0] = norm(z, used[0], R_G2, R_B2, fin_step, 2 * GT * g)
                dve.wait_ge(*used[0])
                b0 = GT * (g % 2)
                x4 = x2_all[:, :].rearrange("p (b j c) -> p b j c", b=B, c=P)[:, b0:b0 + GT, g // 2, :]
                z3 = z.rearrange("p (b c) -> p b c", c=P)
                vec.tensor_tensor(z3, z3, x4, ALU.add).then_inc(fin_done, 1)

            last_scores()
            s0 = softmax(0)
            s1 = softmax(1)
            softmax_norm(0, *s0)
            last_scores_pooled()
            values(0)
            softmax_norm(1, *s1)
            s2 = softmax(2)
            values(1)
            softmax_norm(2, *s2)
            attention_out(0)
            s3 = softmax(3)
            dve.wait_ge(w1_hi_done, 1)
            vec.tensor_tensor(w1_lo[:, :], w1_raw[:, :], w1_hi[:, :].bitcast(F32), ALU.subtract).then_inc(w1_lo_done, 1)
            h_low_part(0)
            route(0)
            softmax_norm(3, *s3)
            attention_out(1)
            values(2)
            h_low_part(1)
            route(1)
            values(3)
            dve.wait_ge(ld_x2, 16)
            dve.wait_ge(x2_kept, 1)
            finish(0)
            attention_out(2)
            h_low_part(2)
            route(2)
            finish(1)
            attention_out(3)
            h_low_part(3)
            route(3)
            finish(2)
            finish(3)

        @block.tensor
        def _(pe):
            mmul = nc.tensor.matmul

            def gate_up(b, n, first):
                e, half = n // 2, n % 2
                if n >= 2 or not first:
                    pe.wait_ge(h_done, b * UNITS + n - 1)
                if n == 0:
                    pe.wait_ge(x_lo_done, b + 1)
                if first and half == 0:
                    pe.wait_ge(w_lo_done, e + 1)
                xh, xl = x_hi[:, bass.ds(b % 2 * T, T)], x_lo[:, bass.ds(b % 2 * T, T)]
                for kind, dst, ready in ((0, pg[n % 2], g_ready), (1, pu[n % 2], u_ready)):
                    if first and half == 0 and kind == 1:
                        pe.wait_ge(w_lo_pool, e + 1)
                    for c in range(2):
                        w = 2 * half + c
                        last = split_matmul(pe, dst[:, c * T:(c + 1) * T], w_part(w_hi, e, kind, w),
                                            w_part(w_lo, e, kind, w), xh, xl, True, True)
                    last.then_inc(ready, 1)

            def down(before, b, m, first=False):
                e, half = m // 2, m % 2
                pe.wait_ge(lo_done, before + m + 1)
                if first and half == 0:
                    pe.wait_ge(wd_lo_pool, e + 1)
                if m == 0 and not isinstance(b, int):
                    pe.wait_ge(cond_lo, b)
                s = (m % 2) * 2 * T
                for c in range(2):
                    w = 2 * half + c
                    last = split_matmul(pe, acc[:, 0:T], w_part(w_hi, e, 2, w), w_part(w_lo, e, 2, w),
                                        h_hi[:, s + c * T:s + (c + 1) * T], h_lo[:, s + c * T:s + (c + 1) * T],
                                        m == 0 and c == 0, m == UNITS - 1 and c == 1)
                last.then_inc(down_done, 1)

            def project(i, dst):
                return split_matmul(pe, dst, p_hi[:, i * P:(i + 1) * P], p_lo[:, i * P:(i + 1) * P],
                                    c_hi[:, :], c_lo[:, :], True, True)

            def spread_v(m):
                dst = (r2, r0)[m % 2]
                for a in range(2):
                    d = 2 * m + a
                    sel = spread_r[:, d * P:(d + 1) * P]
                    mmul(dst[:, a * T:(a + 1) * T], sel, v_hi[:, :], start=True, stop=False)
                    last = mmul(dst[:, a * T:(a + 1) * T], sel, v_lo[:, :], start=False, stop=True)
                last.then_inc(vb_ready, 1)

            def gather_out(pb, m):
                pe.wait_ge(qs_done, 4 * pb + m + 1)
                for a in range(2):
                    d = 2 * m + a
                    last = mmul(r1[:, 0:T], gather_c[:, d * P:(d + 1) * P],
                                state[:, d * T:(d + 1) * T], start=(d == 0), stop=(d == DH - 1))
                return last

            def chain(n, b, pb, middle=False):
                if n == 2:
                    pe.wait_ge(cond_lo, b)
                    for i, dst in ((WK // P, r0[:, 0:T]), (WV // P, r0[:, T:2 * T]), (WQ // P, r1[:, 0:T]),
                                   (WGATE // P, r1[:, T:2 * T])):
                        last = project(i, dst)
                    last.then_inc(kvqg_ready, 1)
                if n == 3:
                    pe.wait_ge(v_lo_done, b)
                    pe.wait_ge(k_done, b)
                    spread_v(0)
                    spread_v(1)
                if n == 4:
                    pe.wait_ge(kv_done, 4 * pb + 1)
                    spread_v(2)
                if n == 5:
                    pe.wait_ge(kv_done, 4 * pb + 2)
                    spread_v(3)
                if n == 6:
                    pe.wait_ge(gate_done, b)
                    gather_out(pb, 0)
                    gather_out(pb, 1)
                if n == 7:
                    gather_out(pb, 2)
                    gather_out(pb, 3).then_inc(cen_ready, 1)
                if n == 8:
                    pe.wait_ge(sq_done, b)
                    for j in range(JT):
                        last = mmul(r2[:, j:j + 1], sqT[:, j * P:(j + 1) * P], mean_col[:, :], start=True, stop=True)
                    last.then_inc(var_ready, 1)
                if n == 11 and middle:
                    pe.wait_ge(rstd_step, b * (RSTEPS + JT))
                    mmul(r2[:, T:2 * T], ones[:, :], diag[:, :], start=True, stop=True).then_inc(bc_ready, 1)
                if n == 12 and middle:
                    pe.wait_ge(ln_step, 2 * b)
                    mmul(r0[:, 0:T], projw[:, WO:WO + P], lnT[:, :], start=True, stop=True).then_inc(wo_ready, 1)
                if n == 12 and not middle:
                    pe.wait_ge(x2_done, b)
                    for j in range(JT):
                        last = nc.tensor.transpose(r1[:, j * P:(j + 1) * P], x2T[:, j * P:(j + 1) * P], ident[:, :])
                    last.then_inc(x2t_ready, 1)
                    mmul(r2[0:A, 0:T], projw[:, WPOOL:WPOOL + A], x2T[:, :], start=True, stop=True).then_inc(pre_ready, 1)
                if n == 13:
                    pe.wait_ge(at_done, b)
                    mmul(r0[:, 0:T], nv_rep[0:A, :], atT[0:A, :], start=True, stop=True).then_inc(s_ready, 1)
                if n == 15:
                    pe.wait_ge(exp_done, JT * pb + JT)
                    for j in range(JT):
                        for l in range(JT):
                            last = nc.tensor.transpose(r1[:, l * T + j * P:l * T + (j + 1) * P],
                                                       ex[:, j * T + l * P:j * T + (l + 1) * P], ident[:, :])
                    last.then_inc(pt_ready, 1)
                if n == 16:
                    pe.wait_ge(pt_done, b)
                    for j in range(JT):
                        for l in range(JT):
                            mmul(r2[:, j * P:(j + 1) * P], pT[:, l * T + j * P:l * T + (j + 1) * P],
                                 x2n[:, l * P:(l + 1) * P], start=(l == 0), stop=(l == JT - 1))
                    for l in range(JT):
                        last = mmul(r0[:, 0:T], x2n[:, l * P:(l + 1) * P], pT[:, l * T:(l + 1) * T],
                                    start=(l == 0), stop=(l == JT - 1))
                    last.then_inc(pooled_ready, 1)
                if n == 17:
                    pe.wait_ge(plT_done, b)
                    pe.wait_ge(pooled_done, JT * pb + JT)
                    for j in range(JT):
                        mmul((r1, r2)[j][:, 0:QKV], plT[:, j * P:(j + 1) * P], projw[:, WIN:WIN + QKV],
                             start=True, stop=True).then_inc(qkv_ready, 1)

            def batch(b, first=False, last=False):
                for n in range(UNITS):
                    if not last:
                        gate_up(b, n, first)
                    if n in (11, 12) and not first:
                        chain(n, b, b - 1, middle=True)
                    if n >= 2 and not last:
                        down(b * UNITS, b, n - 2, first)
                    if n < 2 and not first:
                        down((b - 1) * UNITS, b - 1, UNITS - 2 + n)
                    if not first:
                        chain(n, b, b - 1)

            batch(0, first=True)
            pe.wait_ge(wd_lo_pool, NE)
            pe.wait_ge(p_lo_done, 1)
            pe.wait_ge(spread_done, 1)
            pe.wait_ge(ld_const, 48)
            with pe.Fori(1, B) as b:
                batch(b)
            batch(B, last=True)

            def turn_values(g):
                pe.wait_ge(sum_dve, DVE_SUMS[g])
                pe.wait_ge(sum_pool, sum(len(x) for x in POOL_VALUES[:g + 1]))
                if g >= 1:
                    pe.wait_ge(ctx_done, g)
                for i in range(GT):
                    at = (g % 2) * GC + i * P
                    last = nc.tensor.transpose(pg[0][:, i * P:(i + 1) * P], atn[:, at:at + P], ident[:, :])
                last.then_inc(atT_ready, 1)

            def project_out(g):
                pe.wait_ge(ctx_done, g + 1)
                if g >= 1:
                    pe.wait_ge(y_done, g)
                for i in range(GT):
                    at = (g % 2) * GC + i * P
                    last = mmul(pg[1][:, i * P:(i + 1) * P], ctxT[:, at:at + P], projw[:, WOUT:WOUT + P],
                                start=True, stop=True)
                last.then_inc(proj_ready, 1)

            def turn_h(g):
                for i in range(GT):
                    pe.wait_ge(h_step, 2 * GT * g + GT + i + 1)
                    if g >= 1 and i == 0:
                        pe.wait_ge(hT_done, g)
                    last = nc.tensor.transpose(r1[:, i * P:(i + 1) * P], hn[:, g * GC + i * P:g * GC + (i + 1) * P],
                                               ident[:, :])
                last.then_inc(hT_ready, 1)

            def router(g):
                pe.wait_ge(hT_done, g + 1)
                if g >= 1:
                    pe.wait_ge(ohT_done, 2 * g)
                for i in range(GT):
                    at = (g % 2) * GC + i * P
                    last = mmul(r2[:, i * E:(i + 1) * E], hT[:, at:at + P], projw[:, WROUTE:WROUTE + E],
                                start=True, stop=True)
                last.then_inc(logit_ready, 1)

            def turn_onehot(g):
                pe.wait_ge(onehot_done, g + 1)
                for i in range(GT):
                    last = nc.tensor.transpose(r2[0:E, i * P:(i + 1) * P], onehot[:, i * E:(i + 1) * E], ident[:, :])
                last.then_inc(ohT_ready, 1)

            def expert_in(g, e):
                n = g * E + e
                if n >= 2:
                    pe.wait_ge(gelu_done, n - 1)
                c = slice(e * P, (e + 1) * P)
                own = slice((g % 2) * GC, (g % 2 + 1) * GC)
                split_matmul(pe, pu[n % 2][:, :], w1_hi[:, c], w1_lo[:, c], hT_hi[:, own], hT_lo[:, own], True, False)
                mmul(pu[n % 2][:, :], big_b[0:E, c], ohT_b[0:E, own],
                     start=False, stop=True).then_inc(fpre_ready, 1)

            def expert_out(g, e):
                n = g * E + e
                pe.wait_ge(gelu_done, n + 1)
                for q in range(GT):
                    at = (n % 2) * GC + q * P
                    last = mmul((acc, r0)[g % 2][:, q * P:(q + 1) * P], he[:, at:at + P],
                                w2_sb[:, e * P:(e + 1) * P], start=False, stop=(e == E - 1 and q == GT - 1))
                last.then_inc(he_used, 1)

            def expert_bias(g):
                if g >= 2:
                    pe.wait_ge(z_done, g - 1)
                for q in range(GT):
                    at = (g % 2) * GC + q * P
                    mmul((acc, r0)[g % 2][:, q * P:(q + 1) * P], ohT[0:E, at:at + P], b2_sb[0:E, :],
                         start=(q == 0), stop=False)

            def experts(g):
                pe.wait_ge(ohT_done, 2 * g + 2)
                pe.wait_ge(hT_lo_done, g + 1)
                expert_in(g, 0)
                expert_bias(g)
                for e in range(E):
                    if e + 1 < E:
                        expert_in(g, e + 1)
                    expert_out(g, e)
                    for what, to in BETWEEN.get((g, e), ()):
                        if what == "values":
                            turn_values(to)
                            project_out(to)
                        if what == "h":
                            turn_h(to)
                            router(to)
                        if what == "onehot":
                            turn_onehot(to)

            pe.wait_ge(ld_f, 64)
            turn_values(0)
            project_out(0)
            turn_values(1)
            project_out(1)
            turn_h(0)
            router(0)
            turn_onehot(0)
            pe.wait_ge(w1_lo_done, 1)
            for g in range(GROUPS):
                experts(g)


def bfloat16_bits(constant):
    return (constant.astype(np.float32).view(np.uint32) >> 16).astype(np.uint16)


def shape_constants():
    p, m = np.arange(P)[:, None], np.arange(P)[None, :]
    spread = np.stack([(p == DH * (m // DH) + d) for d in range(DH)], 1).astype(np.float32)
    gather = np.stack([(p // DH == m // DH) & (m % DH == d) for d in range(DH)], 1).astype(np.float32)
    gather -= np.float32(1.0 / P)
    pos = (np.arange(JT)[None, :, None] * P + np.arange(P)[:, None, None])
    l = np.arange(T)[None, None, :]
    masks = bfloat16_bits(np.stack([l > pos, l < pos, l == pos], 1) * BIG)
    consts = np.zeros((P, K_END), np.float32)
    gammas = (1.0 - 2.0 ** (-5.0 - np.arange(H))).repeat(DH)
    consts[:, K_DECAY:K_DECAY + 2 * T] = gammas[:, None]
    consts[:, K_DECAY] = consts[:, K_DECAY + T] = 0.0
    for j in range(JT):
        at = j * P + np.arange(P)
        consts[:, K_CNT + 3 * j], consts[:, K_CNT + 3 * j + 1], consts[:, K_CNT + 3 * j + 2] = at + 1, T - at, T - 1
    consts[:, K_IDX:K_IDX + E] = np.arange(E) + 1
    consts[:, K_TRI:K_TRI + E * E] = (np.arange(E)[None, :] < np.arange(E)[:, None]).reshape(-1)
    big = np.where(np.arange(E)[:, None, None] == np.arange(E)[None, :, None], 0.0, -BIG)
    big = bfloat16_bits(np.broadcast_to(big, (E, E, P)))
    return (spread.reshape(P, -1), gather.reshape(P, -1), np.eye(P, dtype=np.float32), masks.reshape(P, -1),
            consts, np.ascontiguousarray(big).reshape(E, -1))


def kernel(x, fside_Bx8_0, condB_sharedgateprob, itok_B_0_2, **w):
    import concourse.bacc as bacc
    from concourse.bass_utils import run_bass_kernel_spmd

    a = {k: np.asarray(v) for k, v in w.items()}
    gu = [np.concatenate([a["L0_cond_" + n], a["L0_cond_" + s][None]], 0)
          for n, s in (("Wg", "Sg"), ("Wu", "Su"), ("Wd", "Sd"))]
    wd = gu[2].reshape(NE, F // P, P, P).transpose(0, 2, 1, 3).reshape(NE, P, F)
    spread, gather, ident, masks, consts, big = shape_constants()
    arrays = {
        "xT": np.asarray(x).reshape(B * T, P).T,
        "experts": np.concatenate([gu[0], gu[1], wd], 2),
        "proj": np.concatenate([a["L0_attn_Wq"], a["L0_attn_Wk"], a["L0_attn_Wv"], a["L0_attn_Wg"], a["L0_attn_Wo"],
                                a["L0_cond2_W1"], a["L0_ffn_in_proj_w"].T, a["L0_ffn_out_w"].T,
                                a["L0_ffn_router_w"].T], 1),
        "moe_w1": a["L0_ffn_w1"].transpose(2, 0, 1).reshape(P, E * P),
        "moe_w2": a["L0_ffn_w2"].transpose(2, 0, 1).reshape(P, E * P),
        "cols": np.concatenate([a["L0_attn_bg"][:, None], a["L0_attn_bo"][:, None], a["L0_attn_ln_gamma"][:, None],
                                a["L0_attn_ln_beta"][:, None], a["L0_ffn_b1"].T], 1),
        "small": np.stack([a["L0_cond2_b1"], a["L0_cond2_v"]], 1),
        "rows": np.concatenate([a["L0_ffn_in_proj_b"], a["L0_ffn_out_b"], a["L0_ffn_ln1_g"], a["L0_ffn_ln1_b"],
                                a["L0_ffn_ln2_g"], a["L0_ffn_ln2_b"], a["L0_ffn_router_b"]])[None],
        "moe_b2": a["L0_ffn_b2"],
        "fside": np.asarray(fside_Bx8_0).reshape(1, -1),
        "prob": np.asarray(condB_sharedgateprob).reshape(1, -1),
        "itok": np.asarray(itok_B_0_2).reshape(1, -1),
        "spread": spread, "gather": gather, "ident": ident, "masks": masks, "consts": consts, "big": big,
    }
    arrays = {k: np.ascontiguousarray(v) for k, v in arrays.items()}
    nc = bacc.Bacc("TRN2", target_bir_lowering=False, num_devices=1)
    args = [nc.dram_tensor(k, v.shape, mybir.dt.from_np(v.dtype), kind="ExternalInput").ap()
            for k, v in arrays.items()]
    args.append(nc.dram_tensor("out", (B, T, P), F32, kind="ExternalOutput").ap())
    build(nc, *args)
    return run_bass_kernel_spmd(nc, [arrays], core_ids=[0]).results[0]["out"]
```

```python
from contextlib import ExitStack

import numpy as np

import concourse.bass as bass
from concourse import mybir

ALU = mybir.AluOpType
ACT = mybir.ActivationFunctionType
AX = mybir.AxisListType
F32 = mybir.dt.float32
F32R = mybir.dt.float32r
BF16 = mybir.dt.bfloat16
I32 = mybir.dt.int32
U16 = mybir.dt.uint16

P = 128
B = 8
T = 256
JT = T // P
F = 512
NE = 9
UNITS = 2 * NE
H = 16
DH = P // H
E = 8
A = 32
QKV = 3 * P
GROUPS = 4
GT = 4
GC = GT * P
NEWTON = 3
RSTEPS = 3 + 3 * NEWTON
RET_EPS = 1e-3
LN_EPS = 1e-5
HEAD_SCALE = float(DH) ** -0.5
BIG = 1e30
MAGIC = 1597463007.0

WQ, WK, WV, WGATE, WO, WPOOL, WIN, WOUT, WROUTE, WEND = np.cumsum([0, P, P, P, P, P, A, QKV, P, E]).tolist()
C_BG, C_BO, C_GAMMA, C_BETA, C_G1, C_BT1, C_B1 = range(7)
R_INB, R_OUTB, R_G1, R_B1, R_G2, R_B2, R_RB, R_END = np.cumsum([0, QKV, P, P, P, P, P, E]).tolist()
K_DECAY, K_CNT, K_IDX, K_TRI, K_END = np.cumsum([0, 2 * T, 3 * JT, E, E * E]).tolist()


def build(nc, xT, experts, proj, moe_w1, moe_w2, cols, small, rows, moe_b2, fside, prob, itok,
          spread, gather, ident_in, masks, consts, big, out):
    qkvp_dram = nc.dram_tensor("qkvp_scratch", (P, B, JT, QKV + P), F32, kind="Internal").ap()
    x2_dram = nc.dram_tensor("x2_scratch", (P, B, T), F32, kind="Internal").ap()

    with ExitStack() as ctx:
        names = set()

        def sem(name):
            return ctx.enter_context(nc.semaphore(name))

        def bank(name):
            return ctx.enter_context(nc.psum_tensor(name, [P, 512], F32))

        place = {"at": (nc.sbuf_base + 63) // 64 * 64}

        def sb(name, cols_, dt=F32):
            assert name not in names
            names.add(name)
            size = cols_ * (2 if dt == BF16 else 4)
            t = nc.alloc_sbuf_tensor_at(name, [P, cols_], dt, offset=place["at"])
            place["at"] += (size + 63) // 64 * 64
            return t

        ident = sb("ident", P)
        row_bc = sb("row_bc", R_END)
        col = sb("col", C_B1 + E)
        const = sb("const", K_END)
        projw = sb("projw", WEND)

        weights_at = place["at"]
        w_hi = sb("w_hi", NE * 3 * F, F32R)
        w_lo = sb("w_lo", NE * 3 * F, F32R)
        weights_end = place["at"]
        raw_at = place["at"]
        w_raw = sb("w_raw", 2 * 3 * F)
        raw_end = place["at"]
        place["at"] = raw_at
        kv = sb("kv", 2 * 2 * T)
        state_at = place["at"]
        state = sb("state", DH * T)
        place["at"] = state_at
        qs_lo = sb("qs_lo", DH * T, F32R)
        assert place["at"] <= raw_end
        place["at"] = raw_end
        x_sb = sb("x_sb", (B + 1) * T)
        x_hi = sb("x_hi", 2 * T, F32R)
        x_lo = sb("x_lo", 2 * T, F32R)
        masks_sb = sb("masks_sb", 3 * JT * T, BF16)
        mask_now = sb("mask_now", JT * T, BF16)
        mask_part = sb("mask_part", JT * T, BF16)
        spread_r = sb("spread_r", DH * P, F32R)
        gather_r = sb("gather_r", DH * P, F32R)
        h_hi = sb("h_hi", 2 * 2 * T, F32R)
        h_lo = sb("h_lo", 2 * 2 * T, F32R)
        hidden = sb("hidden", 2 * 2 * T)
        small_at = place["at"]
        p_hi = sb("p_hi", 4 * P, F32R)
        p_lo = sb("p_lo", 4 * P, F32R)
        ones = sb("ones", P)
        mean_col = sb("mean_col", 1)
        coef = sb("coef", B * NE)
        cnt = sb("cnt", B * JT)
        fs_bc = sb("fs_bc", B * E)
        pr_bc = sb("pr_bc", B)
        it_bc = sb("it_bc", B, I32)
        itf = sb("itf", B)
        sel_u = sb("sel_u", B)
        sel_l = sb("sel_l", B)
        sel_d = sb("sel_d", B)
        small_sb = sb("small_sb", 2)
        nv_rep = sb("nv_rep", P)
        chain_at = place["at"]
        c_hi = sb("c_hi", T, F32R)
        c_lo = sb("c_lo", T, F32R)
        kT = sb("kT", T)
        v_hi = sb("v_hi", T, F32R)
        v_lo = sb("v_lo", T, F32R)
        qT = sb("qT", T)
        gT = sb("gT", T)
        gammaT = sb("gammaT", T)
        betaT = sb("betaT", T)
        cenT = sb("cenT", T)
        sqT = sb("sqT", T)
        diag = sb("diag", JT * P)
        scaledT = sb("scaledT", T)
        lnT = sb("lnT", T)
        x2T = sb("x2T", T)
        x2n = sb("x2n", T)
        products_at = place["at"]
        atT = sb("atT", T)
        mk = sb("mk", JT * T)
        ex = sb("ex", JT * T)
        pT = sb("pT", JT * T)
        plT = sb("plT", T)
        products_end = place["at"]
        stage = sb("stage", JT * (QKV + P))
        nw = sb("nw", 8 * JT)
        nwi = sb("nwi", 2 * JT, I32)
        mxn = sb("mxn", JT)
        ssum = sb("ssum", JT)
        cnt_now = sb("cnt_now", JT)
        rn = sb("rn", 2 * JT)
        chain_end = place["at"]
        assert chain_end <= nc.sbuf_usable_end, (chain_end, nc.sbuf_usable_end)
        place["at"] = products_at
        qs_hi = sb("qs_hi", DH * T, F32R)
        assert place["at"] <= products_end
        place["at"] = chain_at
        spread_raw = sb("spread_raw", DH * P)
        gather_raw = sb("gather_raw", DH * P)
        w_raw_third = sb("w_raw_third", 3 * F)
        assert place["at"] <= chain_end

        W = QKV + P
        place["at"] = weights_at
        att = [sb(f"att{j}", B * W) for j in range(JT)]
        x2_all = sb("x2_all", B * T)
        w1_raw = sb("w1_raw", E * P)
        w1_hi = sb("w1_hi", E * P, F32R)
        w1_lo = sb("w1_lo", E * P, F32R)
        w2_sb = sb("w2_sb", E * P)
        b2_sb = sb("b2_sb", P)
        big_b = sb("big_b", E * P, BF16)
        ring_dve = sb("ring_dve", 2 * B * P)
        ring_pool = sb("ring_pool", 2 * B * P)
        sc = sb("sc", JT * B * P)
        smx = sb("smx", GROUPS * GT * H)
        ssm = sb("ssm", GROUPS * GT * H)
        resid = sb("resid", GROUPS * GC)
        hn = sb("hn", GROUPS * GC)
        assert place["at"] <= weights_end, (place["at"], weights_end)
        place["at"] = raw_at
        atn = sb("atn", 2 * GC)
        ctxT = sb("ctxT", 2 * GC)
        stats = sb("stats", GT * 6)
        aggr = sb("aggr", GT * 2)
        dev1, off1 = sb("dev1", GROUPS * GT), sb("off1", GROUPS * GT)
        dev2, off2 = sb("dev2", GROUPS * GT), sb("off2", GROUPS * GT)
        nf = sb("nf", 4 * GT)
        nfi = sb("nfi", 2 * GT, I32)
        logit = sb("logit", GT * E)
        r_gt = sb("r_gt", GT * E * E)
        r_eq = sb("r_eq", GT * E * E)
        r_rank = sb("r_rank", GT * E)
        r_val = sb("r_val", GT * E)
        r_max = sb("r_max", GT)
        onehot = sb("onehot", GT * E)
        assert place["at"] <= raw_end
        place["at"] = raw_end
        hT = sb("hT", 2 * GC)
        hT_hi = sb("hT_hi", 2 * GC, F32R)
        hT_lo = sb("hT_lo", 2 * GC, F32R)
        he = sb("he", 2 * GC)
        zf = sb("zf", 2 * GC)
        ohT = sb("ohT", 2 * GC)
        ohT_b = sb("ohT_b", 2 * GC, BF16)
        assert place["at"] <= small_at, (place["at"], small_at)

        pg = [bank("pg0"), bank("pg1")]
        pu = [bank("pu0"), bank("pu1")]
        acc = bank("acc")
        r0, r1, r2 = bank("r0"), bank("r1"), bank("r2")

        ld_x0, ld_x, ld_small, ld_proj, ld_const, ld_masks, ld_spread = (
            sem(n) for n in ("ld_x0", "ld_x", "ld_small", "ld_proj", "ld_const", "ld_masks", "ld_spread"))
        ld_gate0, ld_up0, gate_hi_done = sem("ld_gate0"), sem("ld_up0"), sem("gate_hi_done")
        ld_coef = sem("ld_coef")
        ld_w = [sem(f"ld_w{i}") for i in range(NE)]
        w_hi_done, w_lo_done, w_lo_pool, wd_hi_done, wd_lo_pool = (
            sem(n) for n in ("w_hi_done", "w_lo_done", "w_lo_pool", "wd_hi_done", "wd_lo_pool"))
        x_hi_done, x_lo_done = sem("x_hi_done"), sem("x_lo_done")
        p_hi_done, p_lo_done, spread_done = sem("p_hi_done"), sem("p_lo_done"), sem("spread_done")
        setup_step, setup_dve_step, kinds_done, route_gt = (
            sem(n) for n in ("setup_step", "setup_dve_step", "kinds_done", "route_gt"))
        g_ready, u_ready, silu_done, h_done = sem("g_ready"), sem("u_ready"), sem("silu_done"), sem("h_done")
        hi_done, lo_done, down_done = sem("hi_done"), sem("lo_done"), sem("down_done")
        cond_hi, cond_lo, kvqg_ready = sem("cond_hi"), sem("cond_lo"), sem("kvqg_ready")
        v_hi_done, v_lo_done, k_done, q_done, gate_done = (
            sem(n) for n in ("v_hi_done", "v_lo_done", "k_done", "q_done", "gate_done"))
        gammaT_done, betaT_done, scaled_done = sem("gammaT_done"), sem("betaT_done"), sem("scaled_done")
        vb_ready, kv_done, state_done, qs_done = sem("vb_ready"), sem("kv_done"), sem("state_done"), sem("qs_done")
        ld_gather, gather_done, qs_hi_done, qs_lo_pool, qs_lo_dve = (
            sem(n) for n in ("ld_gather", "gather_done", "qs_hi_done", "qs_lo_pool", "qs_lo_dve"))
        qs_last, qs_lo_last = sem("qs_last"), sem("qs_lo_last")
        cen_ready, cen_done, sq_done, var_ready = sem("cen_ready"), sem("cen_done"), sem("sq_done"), sem("var_ready")
        rstd_step, bc_ready, ln_step, wo_ready = sem("rstd_step"), sem("bc_ready"), sem("ln_step"), sem("wo_ready")
        x2_done, x2t_ready, pre_ready, at_done = sem("x2_done"), sem("x2t_ready"), sem("pre_ready"), sem("at_done")
        x2n_done, s_ready, masked, exp_done = sem("x2n_done"), sem("s_ready"), sem("masked"), sem("exp_done")
        pt_ready, pt_done, pooled_ready, plT_done = (
            sem(n) for n in ("pt_ready", "pt_done", "pooled_ready", "plT_done"))
        rn_step, pooled_done, qkv_ready, qkv_done = sem("rn_step"), sem("pooled_done"), sem("qkv_ready"), sem("qkv_done")
        x2n_sent, qkv_sent, mask_now_done, mask_step, cnt_done = (
            sem(n) for n in ("x2n_sent", "qkv_sent", "mask_now_done", "mask_step", "cnt_done"))
        ld_f, ld_x2, ld_att = sem("ld_f"), sem("ld_x2"), [sem(f"ld_att{j}") for j in range(JT)]
        x2_kept, w1_hi_done, w1_lo_done = sem("x2_kept"), sem("w1_hi_done"), sem("w1_lo_done")
        turned_prod = sem("turned_prod")
        prod_dve, sum_dve, score_pool, sum_pool, tree_pool = (
            sem(n) for n in ("prod_dve", "sum_dve", "score_pool", "sum_pool", "tree_pool"))
        soft_step, norm_step, fexp_done, p_done, resid_done = (
            sem(n) for n in ("soft_step", "norm_step", "fexp_done", "p_done", "resid_done"))
        atT_ready, ctx_done, proj_ready, y_done = sem("atT_ready"), sem("ctx_done"), sem("proj_ready"), sem("y_done")
        stat_step, dev1_done, normal1_done, normal1_dve, h_step, hT_ready, hT_done, hT_hi_done, hT_lo_done = (
            sem(n) for n in ("stat_step", "dev1_done", "normal1_done", "normal1_dve", "h_step", "hT_ready", "hT_done",
                             "hT_hi_done", "hT_lo_done"))
        logit_ready, route_step, onehot_done = sem("logit_ready"), sem("route_step"), sem("onehot_done")
        ohT_b_done = sem("ohT_b_done")
        ohT_ready, ohT_done, fpre_ready, gelu_done = (
            sem(n) for n in ("ohT_ready", "ohT_done", "fpre_ready", "gelu_done"))
        he_used, z_done, dev2_done, normal2_done, normal2_dve, base_done, fin_step, fin_done, last_step, last_done = (
            sem(n) for n in ("he_used", "z_done", "dev2_done", "normal2_done", "normal2_dve", "base_done", "fin_step", "fin_done",
                             "last_step", "last_done"))
        out_sent = [sem(f"out_sent{i}") for i in range(2)]

        block = ctx.enter_context(nc.Block())

        def w_part(tile, e, kind, c):
            at = (e * 3 + kind) * F + c * P
            return tile[:, at:at + P]

        def raw_part(e, first, last):
            if e % 3 == 2:
                return w_raw_third[:, first * F:last * F]
            return w_raw[:, (e % 3 * 3 + first) * F:(e % 3 * 3 + last) * F]

        def split_matmul(pe, dst, l_hi, l_lo, m_hi, m_lo, start, stop):
            pe.matmul(dst, l_hi, m_hi, start=start, stop=False)
            pe.matmul(dst, l_hi, m_lo, start=False, stop=False)
            return pe.matmul(dst, l_lo, m_hi, start=False, stop=stop)

        def att3(j):
            return att[j][:, :].rearrange("p (b c) -> p b c", c=W)

        def sc4(j):
            return sc[:, j * B * P:(j + 1) * B * P].rearrange("p (t s h) -> p t s h", s=B, h=H)

        def slot_of(ring, k):
            return ring[:, (k % 2) * B * P:(k % 2 + 1) * B * P]

        LAST = B - 1
        EARLY_DVE = {7: [(0, 0), (0, 1)], 13: [(0, 5)], 15: [(0, 6)], 16: [(1, 0)]}
        POOL_SCORES = [(0, 2), (0, 3), (0, 4), (1, 1), (1, 3), (1, None), (1, LAST), (1, 6), (1, 5)]

        def pool_scores_before(g):
            own = range(GT * (g % 2), GT * (g % 2) + GT)
            return max([i + 1 for i, (j, t) in enumerate(POOL_SCORES) if j == g // 2 and (t is None or t in own)],
                       default=0)

        POOL_VALUES = [[3], [1, 3], [1, 3], [1, 3]]
        TURNED_SUMS = {0: he, 1: zf}
        sums_until = {}
        BETWEEN = {(0, 0): [("turn_values", 1)], (0, 1): [("project", 1)], (0, 4): [("turn_h", 1)],
                   (0, 5): [("router", 1)], (0, 7): [("turn_onehot", 1)],
                   (1, 0): [("turn_values", 2)], (1, 1): [("project", 2)], (1, 4): [("turn_h", 2)],
                   (1, 5): [("router", 2)], (1, 7): [("turn_onehot", 2)],
                   (2, 0): [("turn_values", 3)], (2, 1): [("project", 3)], (2, 4): [("turn_h", 3)],
                   (2, 5): [("router", 3)], (2, 7): [("turn_onehot", 3)]}
        LATE_EXP = {(0, 1): 2, (0, 7): 3}

        def ahead(g):
            return g + 1 < GROUPS and ("turn_onehot", g + 1) not in BETWEEN.get((g, E - 1), [])

        NORMAL_Z = {(3, 1): 0, (3, 4): 1, (3, 7): 2}

        HIGH_DVE = (13, 14)

        def score_products(eng, slot, j, t, done):
            keys = B if t == LAST else LAST
            out3 = slot[:, 0:keys * P].rearrange("p (s c) -> p s c", c=P)
            if t is None:
                in0, in1 = att3(j)[:, 0:LAST, 0:P], att3(j)[:, LAST, P:2 * P]
            else:
                in0, in1 = att3(j)[:, 0:keys, P:2 * P], att3(j)[:, t, 0:P]
            eng.tensor_tensor(out3, in0, in1.unsqueeze(1).broadcast_to((P, keys, P)), ALU.mult).then_inc(done, 1)

        def scores_at(j, t):
            if t is None:
                return sc4(j)[:, 0:LAST, LAST, :]
            return sc4(j)[:, t, 0:(B if t == LAST else LAST), :]

        def wait_for_qk(eng, j, t):
            if t is None or t == LAST:
                eng.wait_ge(qkv_done, JT * LAST + j + 1)
            eng.wait_ge(ld_att[j], 16)

        def product_low(eng, waits, pb, m, done):
            waits.wait_ge(qs_hi_done, 4 * pb + m + 1)
            c = slice(m * 512, m * 512 + 512)
            eng.tensor_tensor(qs_lo[:, c], state[:, c], qs_hi[:, c].bitcast(F32),
                              ALU.subtract).then_inc(done, 1)

        def x2_part(g):
            b0 = GT * (g % 2)
            return x2_all[:, :].rearrange("p (b j c) -> p b j c", b=B, c=P)[:, b0:b0 + GT, g // 2, :]

        def value_products(eng, slot, g, i, done):
            j, t = g // 2, GT * (g % 2) + i
            eng.tensor_tensor(slot.rearrange("p (s h d) -> p s h d", h=H, d=DH),
                              att3(j)[:, :, 2 * P:3 * P].rearrange("p s (h d) -> p s h d", d=DH),
                              sc4(j)[:, t].unsqueeze(3).broadcast_to((P, B, H, DH)), ALU.mult).then_inc(done, 1)

        @block.sync
        def _(sp):
            sp.dma_start(x_sb[:, 0:T], xT[:, 0:T]).then_inc(ld_x0, 16)

            def load_expert(e):
                if e >= 3:
                    sp.wait_ge(w_lo_done, e - 2)
                    sp.wait_ge(wd_lo_pool, e - 2)
                sp.dma_start(raw_part(e, 0, 3), experts[e]).then_inc(ld_w[e], 16)

            for kind, done in enumerate((ld_gate0, ld_up0, ld_w[0])):
                sp.dma_start(w_raw[:, kind * F:(kind + 1) * F], experts[0, :, kind * F:(kind + 1) * F]).then_inc(done, 16)
            sp.dma_start(fs_bc[:, :], fside.broadcast_to((P, B * E))).then_inc(ld_coef, 16)
            sp.dma_start(pr_bc[:, :], prob.broadcast_to((P, B))).then_inc(ld_coef, 16)
            load_expert(1)
            load_expert(2)
            sp.dma_start(projw[:, :], proj).then_inc(ld_proj, 16)
            load_expert(3)
            sp.dma_start(x_sb[:, T:B * T], xT[:, T:B * T]).then_inc(ld_x, 16)
            sp.dma_start(x_sb[:, B * T:(B + 1) * T], xT[:, 0:T]).then_inc(ld_x, 16)
            load_expert(4)
            sp.dma_start(it_bc[:, :], itok.broadcast_to((P, B))).then_inc(ld_small, 16)
            sp.dma_start(col[:, :], cols).then_inc(ld_small, 16)
            sp.dma_start(const[:, :], consts).then_inc(ld_small, 16)
            sp.dma_start(small_sb[0:A, :], small).then_inc(ld_small, 16)
            sp.dma_start(spread_raw[:, :], spread).then_inc(ld_spread, 16)
            load_expert(5)
            sp.dma_start(gather_raw[:, :], gather).then_inc(ld_gather, 16)
            sp.dma_start(masks_sb[:, :].bitcast(U16), masks).then_inc(ld_masks, 16)
            load_expert(6)
            sp.dma_start(ident[:, :], ident_in).then_inc(ld_const, 16)
            sp.dma_start(row_bc[:, :], rows.broadcast_to((P, R_END))).then_inc(ld_const, 16)
            for e in range(7, NE):
                load_expert(e)

            def store_batch(pb):
                row = slice(pb, pb + 1)
                sp.wait_ge(x2n_done, pb + 1)
                sp.dma_start(x2_dram[:, row, :], x2n[:, :].unsqueeze(1)).then_inc(x2n_sent, 16)
                sp.wait_ge(pooled_done, 2 * pb + 2)
                sp.wait_ge(qkv_done, 2 * pb + 2)
                sp.dma_start(qkvp_dram[:, row, :, :],
                             stage[:, :].rearrange("p (j c) -> p j c", j=JT).unsqueeze(1)).then_inc(qkv_sent, 16)
                sp.wait_ge(qkv_sent, 16 * pb + 16)

            for pb in range(B - 1):
                store_batch(pb)
            sp.wait_ge(down_done, B * UNITS)
            for j in range(JT):
                sp.dma_start(att[j][:, 0:LAST * W].rearrange("p (b c) -> p b c", c=W),
                             qkvp_dram[:, 0:LAST, j, :]).then_inc(ld_att[j], 16)
            sp.dma_start(w1_raw[:, :], moe_w1).then_inc(ld_f, 16)
            sp.dma_start(w2_sb[:, :], moe_w2).then_inc(ld_f, 16)
            sp.dma_start(b2_sb[0:E, :], moe_b2).then_inc(ld_f, 16)
            sp.dma_start(big_b[0:E, :].bitcast(U16), big).then_inc(ld_f, 16)
            sp.dma_start(x2_all[:, 0:LAST * T].rearrange("p (b c) -> p b c", c=T),
                         x2_dram[:, 0:LAST, :]).then_inc(ld_x2, 16)
            for g in range(GROUPS):
                j, b0 = g // 2, GT * (g % 2)
                if g + 1 < GROUPS:
                    sp.wait_ge(fin_done, g + 1)
                else:
                    sp.wait_ge(last_done, GT)
                sp.dma_start(out[b0:b0 + GT, j * P:(j + 1) * P, :].rearrange("b p c -> p b c"),
                             zf[:, (g % 2) * GC:(g % 2 + 1) * GC].rearrange("p (b c) -> p b c", c=P))\
                    .then_inc(out_sent[g % 2], 16)
            for i in range(2):
                sp.wait_ge(out_sent[i], 16 * GROUPS // 2)

        @block.gpsimd
        def _(pool):
            nc.gpsimd.memset(ones[:, :], 1.0).then_inc(setup_step, 1)
            nc.gpsimd.memset(mean_col[:, :], 1.0 / P).then_inc(setup_step, 1)
            for e in range(NE):
                for kind, hi_ready, done in ((1, w_hi_done, w_lo_pool), (2, wd_hi_done, wd_lo_pool)):
                    pool.wait_ge(hi_ready, e + 1)
                    a = (e * 3 + kind) * F
                    nc.gpsimd.tensor_tensor(w_lo[:, a:a + F], raw_part(e, kind, kind + 1),
                                            w_hi[:, a:a + F].bitcast(F32), ALU.subtract).then_inc(done, 1)

            def query_states(pb, last=False):
                pool.wait_ge(q_done, pb + 1)
                for m in range(3 if last else 4):
                    pool.wait_ge(state_done, 4 * pb + m + 1)
                    s = state[:, m * 512:m * 512 + 512].rearrange("p (a t) -> p a t", a=2)
                    nc.gpsimd.tensor_tensor(s, s, qT[:, :].unsqueeze(1).broadcast_to((P, 2, T)),
                                            ALU.mult).then_inc(qs_done, 1)
                    if m == 0 and not last:
                        product_low(nc.gpsimd, pool, pb, m, qs_lo_pool)

            def scale_norm(pb):
                pool.wait_ge(cen_done, pb + 1)
                pool.wait_ge(gammaT_done, pb + 1)
                nc.gpsimd.tensor_tensor(scaledT[:, :], cenT[:, :], gammaT[:, :], ALU.mult).then_inc(scaled_done, 1)

            def mask_of(pb):
                step = mask_step_of(pb)
                for k, kind in enumerate((sel_u, sel_l, sel_d)):
                    part = mask_now if k == 0 else mask_part
                    step(nc.gpsimd.tensor_tensor(part[:, :], masks_sb[:, k * JT * T:(k + 1) * JT * T],
                                                 kind[:, bass.ds(pb, 1)].broadcast_to((P, JT * T)), ALU.mult))
                    if k == 1:
                        step(nc.gpsimd.tensor_tensor(mask_now[:, :], mask_now[:, :], mask_part[:, :], ALU.add))
                nc.gpsimd.tensor_tensor(mask_now[:, :], mask_now[:, :], mask_part[:, :],
                                        ALU.add).then_inc(mask_now_done, 1)

            def mask_step_of(pb):
                k = [0]

                def step(ins):
                    k[0] += 1
                    ins.then_inc(mask_step, 1)
                    pool.wait_ge(mask_step, pb * 4 + k[0])
                return step

            pool.wait_ge(ld_masks, 16)
            pool.wait_ge(kinds_done, 1)
            with pool.Fori(0, LAST) as pb:
                query_states(pb)
                mask_of(pb)
                scale_norm(pb)
            query_states(LAST, last=True)
            mask_of(LAST)
            scale_norm(LAST)

            used = [0]
            halved = [0]

            def halve(out_ap, a, b_, done):
                pool.wait_ge(tree_pool, halved[0])
                nc.gpsimd.tensor_tensor(out_ap, a, b_, ALU.add).then_inc(done, 1)
                if done is tree_pool:
                    halved[0] += 1

            def free_slot():
                slot = slot_of(ring_pool, used[0])
                used[0] += 1
                return slot

            def scores(i):
                j, t = POOL_SCORES[i]
                wait_for_qk(pool, j, t)
                if i >= 2:
                    pool.wait_ge(score_pool, i - 1)
                slot = free_slot()
                score_products(nc.gpsimd, slot, j, t, tree_pool)
                halved[0] += 1
                n = B if t == LAST else LAST
                v = slot[:, 0:n * P].rearrange("p (a d) -> p a d", d=DH)
                halve(v[:, :, 0:4], v[:, :, 0:4], v[:, :, 4:8], tree_pool)
                halve(v[:, :, 0:2], v[:, :, 0:2], v[:, :, 2:4], tree_pool)
                v = v.rearrange("p (s h) d -> p s h d", h=H)
                halve(scores_at(j, t), v[:, :, :, 0], v[:, :, :, 1], score_pool)

            def residual(g):
                j, b0 = g // 2, GT * (g % 2)
                pool.wait_ge(pooled_done, JT * B if g % 2 else JT * LAST)
                pool.wait_ge(ld_att[j], 16)
                nc.gpsimd.tensor_tensor(resid[:, g * GC:(g + 1) * GC].rearrange("p (b c) -> p b c", c=P),
                                        att3(j)[:, b0:b0 + GT, QKV:W],
                                        row_bc[:, R_OUTB:R_OUTB + P].unsqueeze(1).broadcast_to((P, GT, P)),
                                        ALU.add).then_inc(resid_done, 1)

            def values(g):
                pool.wait_ge(p_done, g + 1)
                pool.wait_ge(score_pool, scored)
                if g >= 2:
                    pool.wait_ge(atT_ready, g - 1)
                for k, i in enumerate(POOL_VALUES[g]):
                    before = sum(len(x) for x in POOL_VALUES[:g]) + k
                    if before >= 1:
                        pool.wait_ge(sum_pool, before)
                    slot = free_slot()
                    value_products(nc.gpsimd, slot, g, i, tree_pool)
                    halved[0] += 1
                    halve(slot[:, 0:4 * P], slot[:, 0:4 * P], slot[:, 4 * P:8 * P], tree_pool)
                    halve(slot[:, 0:2 * P], slot[:, 0:2 * P], slot[:, 2 * P:4 * P], tree_pool)
                    at = (g % 2) * GC + i * P
                    halve(atn[:, at:at + P], slot[:, 0:P], slot[:, P:2 * P], sum_pool)

            def rows4(buf, g):
                return buf[:, g * GC:(g + 1) * GC].rearrange("p (b c) -> p b c", c=P)

            def row4(at):
                return row_bc[:, at:at + P].unsqueeze(1).broadcast_to((P, GT, P))

            def scale_h(g):
                pool.wait_ge(hT_ready, g + 1)
                nc.gpsimd.tensor_tensor(rows4(hn, g), rows4(hn, g), row4(R_G1), ALU.mult).then_inc(h_step, 1)
                pool.wait_ge(h_step, 2 * g + 1)
                nc.gpsimd.tensor_tensor(rows4(hn, g), rows4(hn, g), row4(R_B1), ALU.add).then_inc(h_step, 1)

            def base(g):
                pool.wait_ge(ld_x2, 16)
                pool.wait_ge(x2_kept, 1)
                x4 = x2_part(g)
                nc.gpsimd.tensor_tensor(x4, x4, row4(R_B2), ALU.add).then_inc(base_done, 1)

            def finish(g):
                z3 = rows4(zf, g % 2)
                pool.wait_ge(normal2_done, GT // 2 * (g + 1))
                pool.wait_ge(normal2_dve, GT // 2 * (g + 1))
                nc.gpsimd.tensor_tensor(z3, z3, row4(R_G2), ALU.mult).then_inc(fin_step, 1)
                pool.wait_ge(fin_step, g + 1)
                pool.wait_ge(base_done, g + 1)
                nc.gpsimd.tensor_tensor(z3, z3, x2_part(g), ALU.add).then_inc(fin_done, 1)

            scored = 0
            for i in range(4):
                scores(i)
            scored = 4
            pool.wait_ge(w1_hi_done, 1)
            nc.gpsimd.tensor_tensor(w1_lo[:, :], w1_raw[:, :], w1_hi[:, :].bitcast(F32), ALU.subtract).then_inc(w1_lo_done, 1)
            residual(0)
            values(0)
            residual(1)
            scores(4)
            scores(5)
            scores(6)
            scored = 7
            values(1)
            scores(7)
            scores(8)
            scored = 9
            values(2)
            scale_h(0)
            residual(2)
            values(3)
            residual(3)
            scale_h(1)
            scale_h(2)
            pool.wait_ge(x2n_done, B)
            nc.gpsimd.tensor_copy(x2_all[:, LAST * T:B * T], x2n[:, :]).then_inc(x2_kept, 1)
            for g in range(GROUPS):
                base(g)
            scale_h(3)
            for g in range(GROUPS - 1):
                finish(g)

        @block.scalar
        def _(act):
            def split_gate(e):
                act.wait_ge(ld_gate0 if e == 0 else ld_w[e], 16)
                nc.scalar.activation(w_hi[:, e * 3 * F:(e * 3 + 1) * F], raw_part(e, 0, 1),
                                     ACT.Copy).then_inc(gate_hi_done, 1)

            def split_up(e):
                act.wait_ge(ld_up0 if e == 0 else ld_w[e], 16)
                nc.scalar.activation(w_hi[:, (e * 3 + 1) * F:(e * 3 + 2) * F], raw_part(e, 1, 2),
                                     ACT.Copy).then_inc(w_hi_done, 1)

            def split_x(b):
                nc.scalar.activation(x_hi[:, bass.ds(b % 2 * T, T)], x_sb[:, bass.ds(b * T, T)],
                                     ACT.Copy).then_inc(x_hi_done, 1)

            def h_high(done, m):
                act.wait_ge(h_done, done + m + 1)
                if not (isinstance(done, int) and done + m < 2):
                    act.wait_ge(down_done, done + m - 1)
                s = (m % 2) * 2 * T
                nc.scalar.activation(h_hi[:, s:s + 2 * T], hidden[:, s:s + 2 * T], ACT.Copy).then_inc(hi_done, 1)

            def product_high(pb, m, last=False):
                if last and m == 3:
                    act.wait_ge(qs_last, 1)
                else:
                    act.wait_ge(qs_done, 4 * pb + m + 1)
                c = slice(m * 512, m * 512 + 512)
                nc.scalar.activation(qs_hi[:, c], state[:, c], ACT.Copy).then_inc(qs_hi_done, 1)

            def exponentials(pb):
                for j in range(JT):
                    act.wait_ge(masked, JT * pb + j + 1)
                    nc.scalar.activation(ex[:, j * T:(j + 1) * T], mk[:, j * T:(j + 1) * T], ACT.Exp,
                                         bias=mxn[:, j:j + 1], scale=-1.0,
                                         accum_out=ssum[:, j:j + 1]).then_inc(exp_done, 1)

            def chain(n, b, pb, last):
                if n == 2:
                    act.wait_ge(down_done, b * UNITS)
                    nc.scalar.activation(c_hi[:, :], acc[:, 0:T], ACT.Copy).then_inc(cond_hi, 1)
                if n == 3:
                    act.wait_ge(kvqg_ready, b)
                    nc.scalar.activation(v_hi[:, :], r0[:, T:2 * T], ACT.Copy).then_inc(v_hi_done, 1)
                    nc.scalar.activation(kT[:, :], r0[:, 0:T], ACT.Copy).then_inc(k_done, 1)
                if n == 4:
                    nc.scalar.activation(qT[:, :], r1[:, 0:T], ACT.Copy, scale=HEAD_SCALE).then_inc(q_done, 1)
                    nc.scalar.activation(gT[:, :], r1[:, T:2 * T], ACT.Silu,
                                         bias=col[:, C_BG:C_BG + 1]).then_inc(gate_done, 1)
                if n == 5:
                    act.wait_ge(gate_done, b)
                    nc.scalar.activation(gammaT[:, :], gT[:, :], ACT.Copy,
                                         scale=col[:, C_GAMMA:C_GAMMA + 1]).then_inc(gammaT_done, 1)
                    nc.scalar.activation(betaT[:, :], gT[:, :], ACT.Copy,
                                         scale=col[:, C_BETA:C_BETA + 1]).then_inc(betaT_done, 1)
                    product_high(pb, 0)
                if n == 7:
                    product_high(pb, 2)
                    product_high(pb, 3, last)
                if n == 8:
                    act.wait_ge(cen_ready, b)
                    nc.scalar.activation(cenT[:, :], r1[:, 0:T], ACT.Copy).then_inc(cen_done, 1)
                    nc.scalar.activation(sqT[:, :], r1[:, 0:T], ACT.Square).then_inc(sq_done, 1)
                if n == 10 and last:
                    act.wait_ge(ld_f, 64)
                    nc.scalar.activation(w1_hi[:, :], w1_raw[:, :], ACT.Copy).then_inc(w1_hi_done, 1)
                if n == 13:
                    act.wait_ge(pre_ready, b)
                    nc.scalar.activation(atT[0:A, :], r2[0:A, 0:T], ACT.Tanh,
                                         bias=small_sb[0:A, 0:1]).then_inc(at_done, 1)
                    act.wait_ge(x2t_ready, b)
                    nc.scalar.activation(x2n[:, :], r1[:, 0:T], ACT.Copy).then_inc(x2n_done, 1)
                if n == 17:
                    act.wait_ge(pooled_ready, b)
                    nc.scalar.activation(plT[:, :], r0[:, 0:T], ACT.Copy).then_inc(plT_done, 1)
                if n == 17 and not last:
                    act.wait_ge(x2n_sent, 16 * b)

            def batch(b, first=False, last=False):
                for n in range(UNITS):
                    if not first:
                        chain(n, b, b - 1, last)
                    ahead = not first and n == 9
                    if ahead and not last:
                        h_high(b * UNITS, n - 1)
                    if not last:
                        act.wait_ge(g_ready, b * UNITS + n + 1)
                        if n >= 2 or not first:
                            act.wait_ge(lo_done, b * UNITS + n - 1)
                        s = (n % 2) * 2 * T
                        nc.scalar.activation(hidden[:, s:s + 2 * T], pg[n % 2][:, :], ACT.Silu).then_inc(silu_done, 1)
                        if n == 12:
                            if first:
                                act.wait_ge(ld_x, 32)
                            split_x(b + 1)
                    if n == 14 and not first:
                        exponentials(b - 1)
                    if n >= 1 and not last and not ahead and (first or n - 1 not in HIGH_DVE):
                        h_high(b * UNITS, n - 1)
                    if n == 6 and not first:
                        product_high(b - 1, 1)
                    if n == 0 and not first:
                        h_high((b - 1) * UNITS, UNITS - 1)
                    if first:
                        if n % 2 == 0 and n // 2 + 1 < NE:
                            split_gate(n // 2 + 1)
                        if n == 0:
                            split_up(1)
                        if n % 2 == 1 and (n + 3) // 2 < NE:
                            split_up((n + 3) // 2)
                        if n == 5:
                            act.wait_ge(ld_proj, 16)
                            nc.scalar.activation(p_hi[:, :], projw[:, 0:4 * P], ACT.Copy).then_inc(p_hi_done, 1)
                        if n == 13:
                            act.wait_ge(ld_gather, 16)
                            nc.scalar.activation(gather_r[:, :], gather_raw[:, :], ACT.Copy).then_inc(gather_done, 1)
                        if n == 11:
                            act.wait_ge(ld_spread, 16)
                            nc.scalar.activation(spread_r[:, :], spread_raw[:, :], ACT.Copy).then_inc(spread_done, 1)

            act.wait_ge(ld_x0, 16)
            split_x(0)
            split_gate(0)
            split_up(0)
            batch(0, first=True)
            with act.Fori(1, B) as b:
                batch(b)
            batch(B, last=True)

            def softmax_exp(g):
                j, a = g // 2, g * GC
                act.wait_ge(soft_step, 2 * g + 2)
                nc.scalar.activation(sc[:, a:a + GC], sc[:, a:a + GC], ACT.Exp, scale=HEAD_SCALE).then_inc(fexp_done, 1)

            def values_copy(g):
                act.wait_ge(atT_ready, g + 1)
                nc.scalar.activation(ctxT[:, (g % 2) * GC:(g % 2 + 1) * GC], pg[0][:, :], ACT.Copy).then_inc(ctx_done, 1)

            def normal_h(g):
                act.wait_ge(dev1_done, 2 * g + 2)
                for t in range(GT // 2):
                    k, c = g * GT + t, slice(g * GC + t * P, g * GC + t * P + P)
                    nc.scalar.activation(hn[:, c], hn[:, c], ACT.Identity, bias=off1[:, k:k + 1],
                                         scale=dev1[:, k:k + 1]).then_inc(normal1_done, 1)

            def h_copy(g):
                act.wait_ge(hT_ready, g + 1)
                if g >= 2:
                    act.wait_ge(fpre_ready, E * (g - 1))
                c = slice((g % 2) * GC, (g % 2 + 1) * GC)
                for dst, done in ((hT, hT_done), (hT_hi, hT_hi_done)):
                    nc.scalar.activation(dst[:, c], r1[:, :], ACT.Identity, bias=col[:, C_BT1:C_BT1 + 1],
                                         scale=col[:, C_G1:C_G1 + 1]).then_inc(done, 1)

            def normal_z(g):
                act.wait_ge(dev2_done, 2 * g + 2)
                for t in range(GT // 2):
                    k, c = g * GT + t, slice((g % 2) * GC + t * P, (g % 2) * GC + t * P + P)
                    nc.scalar.activation(zf[:, c], zf[:, c], ACT.Identity, bias=off2[:, k:k + 1],
                                         scale=dev2[:, k:k + 1]).then_inc(normal2_done, 1)

            def onehot_copy(g):
                act.wait_ge(ohT_ready, g + 1)
                c = slice((g % 2) * GC, (g % 2 + 1) * GC)
                nc.scalar.activation(ohT_b[0:E, c], r2[0:E, :], ACT.Copy).then_inc(ohT_b_done, 1)
                nc.scalar.activation(ohT[0:E, c], r2[0:E, :], ACT.Copy).then_inc(ohT_done, 1)

            def expert_gelu(g, e):
                n = g * E + e
                act.wait_ge(fpre_ready, n + 1)
                if n >= 2:
                    act.wait_ge(he_used, n - 1)
                nc.scalar.activation(he[:, (n % 2) * GC:(n % 2 + 1) * GC], pu[n % 2][:, :], ACT.Gelu,
                                     bias=col[:, C_B1 + e:C_B1 + e + 1]).then_inc(gelu_done, 1)

            softmax_exp(0)
            values_copy(0)
            softmax_exp(1)
            normal_h(0)
            h_copy(0)
            onehot_copy(0)
            for g in range(GROUPS):
                for e in range(E):
                    expert_gelu(g, e)
                    for what, to in BETWEEN.get((g, e), ()):
                        if what == "turn_h":
                            normal_h(to)
                    if (g, e) in LATE_EXP:
                        softmax_exp(LATE_EXP[g, e])
                    work = BETWEEN.get((g, e - 1), []) + (BETWEEN.get((g, e), []) if e == E - 1 else [])
                    for what, to in work:
                        if what == "turn_values":
                            values_copy(to)
                        if what == "turn_h":
                            h_copy(to)
                        if what == "turn_onehot":
                            onehot_copy(to)
                    if (g, e) in NORMAL_Z:
                        normal_z(NORMAL_Z[g, e])
            normal_z(GROUPS - 1)

        @block.vector
        def _(dve):
            vec = nc.vector

            count = [0]

            def step(ins):
                count[0] += 1
                ins.then_inc(setup_dve_step, 1)
                dve.wait_ge(setup_dve_step, count[0])

            def split_x(b):
                dve.wait_ge(x_hi_done, b + 1)
                vec.tensor_tensor(x_lo[:, bass.ds(b % 2 * T, T)], x_sb[:, bass.ds(b * T, T)],
                                  x_hi[:, bass.ds(b % 2 * T, T)].bitcast(F32), ALU.subtract).then_inc(x_lo_done, 1)

            def gate_low(e):
                dve.wait_ge(gate_hi_done, e + 1)
                a = e * 3 * F
                vec.tensor_tensor(w_lo[:, a:a + F], raw_part(e, 0, 1),
                                  w_hi[:, a:a + F].bitcast(F32), ALU.subtract).then_inc(w_lo_done, 1)

            def down_high(e):
                dve.wait_ge(ld_w[e], 16)
                a = (e * 3 + 2) * F
                vec.tensor_copy(w_hi[:, a:a + F], raw_part(e, 2, 3)).then_inc(wd_hi_done, 1)

            def setup(n):
                if n == 13:
                    dve.wait_ge(ld_small, 64)
                    step(vec.tensor_copy(itf[:, :], it_bc[:, :]))
                    step(vec.tensor_scalar(sel_u[:, :], itf[:, :], 0.0, None, ALU.is_equal))
                    step(vec.tensor_scalar(sel_l[:, :], itf[:, :], 1.0, None, ALU.is_equal))
                    step(vec.tensor_tensor(sel_d[:, :], sel_u[:, :], sel_l[:, :], ALU.add))
                if n == 14:
                    step(vec.tensor_scalar(sel_d[:, :], sel_d[:, :], -1.0, 1.0, ALU.mult, ALU.add))
                    vec.tensor_copy(itf[:, :], sel_d[:, :]).then_inc(kinds_done, 1)
                if n in (15, 16):
                    j = n - 15
                    c = cnt[:, :].rearrange("p (b j) -> p b j", j=JT)[:, :, j]
                    k = K_CNT + 3 * j
                    step(vec.tensor_scalar(c, sel_u[:, :], const[:, k:k + 1], None, ALU.mult))
                    step(vec.scalar_tensor_tensor(out=c, in0=sel_l[:, :], scalar=const[:, k + 1:k + 2], in1=c,
                                                  op0=ALU.mult, op1=ALU.add))
                    step(vec.scalar_tensor_tensor(out=c, in0=sel_d[:, :], scalar=const[:, k + 2:k + 3], in1=c,
                                                  op0=ALU.mult, op1=ALU.add))
                if n == 17:
                    step(vec.tensor_scalar(nv_rep[0:A, :], ones[0:A, :], small_sb[0:A, 1:2], -1.0,
                                           ALU.mult, ALU.mult))
                if n == 5:
                    dve.wait_ge(p_hi_done, 1)
                    vec.tensor_tensor(p_lo[:, :], projw[:, 0:4 * P], p_hi[:, :].bitcast(F32),
                                      ALU.subtract).then_inc(p_lo_done, 1)

            def h_low(done, m):
                dve.wait_ge(hi_done, done + m + 1)
                s = (m % 2) * 2 * T
                vec.tensor_tensor(h_lo[:, s:s + 2 * T], hidden[:, s:s + 2 * T], h_hi[:, s:s + 2 * T].bitcast(F32),
                                  ALU.subtract).then_inc(lo_done, 1)

            def h_high(done, m):
                dve.wait_ge(h_done, done + m + 1)
                dve.wait_ge(down_done, done + m - 1)
                s = (m % 2) * 2 * T
                vec.tensor_copy(h_hi[:, s:s + 2 * T], hidden[:, s:s + 2 * T]).then_inc(hi_done, 1)

            def hidden_values(b, n):
                dve.wait_ge(silu_done, b * UNITS + n + 1)
                dve.wait_ge(u_ready, b * UNITS + n + 1)
                s = (n % 2) * 2 * T
                vec.scalar_tensor_tensor(out=hidden[:, s:s + 2 * T], in0=hidden[:, s:s + 2 * T],
                                         scalar=coef[:, bass.ds(b * NE + n // 2, 1)], in1=pu[n % 2][:, :],
                                         op0=ALU.mult, op1=ALU.mult).then_inc(h_done, 1)

            def guess(steps, src, eps, w, wi, n):
                v = w[:, 0:n]
                steps(vec.tensor_scalar(v, src, eps, None, ALU.add))
                steps(vec.tensor_scalar(wi[:, 0:n], v.bitcast(I32), 1, None, ALU.logical_shift_right))
                steps(vec.tensor_scalar(wi[:, n:2 * n], wi[:, 0:n], -1.0, MAGIC, ALU.mult, ALU.add))
                return wi[:, n:2 * n].bitcast(F32)

            def newton(steps, g_in, w, n, times):
                v, g, a = w[:, 0:n], w[:, n:2 * n], w[:, 2 * n:3 * n]
                for _ in range(times):
                    steps(vec.scalar_tensor_tensor(out=a, in0=g_in, scalar=-0.5, in1=g_in, op0=ALU.mult, op1=ALU.mult))
                    steps(vec.tensor_tensor(a, a, v, ALU.mult))
                    steps(vec.scalar_tensor_tensor(out=g, in0=a, scalar=1.5, in1=g_in, op0=ALU.add, op1=ALU.mult))
                    g_in = g
                return g

            def rsqrt(steps, src, eps, w, wi, n):
                return newton(steps, guess(steps, src, eps, w, wi, n), w, n, NEWTON)

            def stepper(semaphore, base):
                k = [0]

                def run(ins):
                    k[0] += 1
                    ins.then_inc(semaphore, 1)
                    dve.wait_ge(semaphore, base + k[0])
                return run

            def scan(m):
                s = (m % 2) * 2 * T
                vec.tensor_tensor_scan(state[:, m * 512:m * 512 + 512], const[:, K_DECAY:K_DECAY + 512],
                                       kv[:, s:s + 512], 0.0, ALU.mult, ALU.add).then_inc(state_done, 1)

            def outer(pb, m):
                dve.wait_ge(vb_ready, 4 * pb + m + 1)
                s = (m % 2) * 2 * T
                src = (r2, r0)[m % 2]
                vec.tensor_tensor(kv[:, s:s + 512].rearrange("p (a t) -> p a t", a=2),
                                  src[:, :].rearrange("p (a t) -> p a t", a=2),
                                  kT[:, :].unsqueeze(1).broadcast_to((P, 2, T)), ALU.mult).then_inc(kv_done, 1)

            def gated_norm(b, pb):
                dve.wait_ge(bc_ready, b)
                dve.wait_ge(scaled_done, b)
                dve.wait_ge(betaT_done, b)
                st = stepper(ln_step, pb * 2)
                st(vec.tensor_tensor(lnT[:, :], scaledT[:, :], r2[:, T:2 * T], ALU.mult))
                st(vec.tensor_tensor(lnT[:, :], lnT[:, :], betaT[:, :], ALU.add))

            def rstd_begin(b, pb):
                dve.wait_ge(var_ready, b)
                st = stepper(rstd_step, pb * (RSTEPS + JT))
                newton(st, guess(st, r2[:, 0:JT], RET_EPS, nw, nwi, JT), nw, JT, 1)

            def rstd_end(pb):
                g = newton(stepper(rstd_step, pb * (RSTEPS + JT) + 6), nw[:, JT:2 * JT], nw, JT, NEWTON - 1)
                for j in range(JT):
                    vec.tensor_scalar(diag[:, j * P:(j + 1) * P], ident[:, :], g[:, j:j + 1], None,
                                      ALU.mult).then_inc(rstd_step, 1)

            def store_qkv(b, pb, j, last):
                dve.wait_ge(qkv_ready, JT * pb + j + 1)
                dst = att[j][:, LAST * W:B * W] if last else stage[:, j * W:(j + 1) * W]
                vec.scalar_tensor_tensor(out=dst[:, 0:QKV], in0=(r1, r2)[j][:, 0:QKV],
                                         scalar=rn[:, JT + j:JT + j + 1], in1=row_bc[:, R_INB:R_INB + QKV],
                                         op0=ALU.mult, op1=ALU.add).then_inc(qkv_done, 1)

            def chain(n, b, pb, last):
                if n == 2:
                    dve.wait_ge(cond_hi, b)
                    vec.tensor_tensor(c_lo[:, :], acc[:, 0:T], c_hi[:, :].bitcast(F32),
                                      ALU.subtract).then_inc(cond_lo, 1)
                if n == 3:
                    dve.wait_ge(v_hi_done, b)
                    dve.wait_ge(k_done, b)
                    vec.tensor_tensor(v_lo[:, :], r0[:, T:2 * T], v_hi[:, :].bitcast(F32),
                                      ALU.subtract).then_inc(v_lo_done, 1)
                if n == 4:
                    outer(pb, 0)
                    outer(pb, 1)
                    dve.wait_ge(kv_done, 4 * pb + 1)
                    scan(0)
                if n == 5:
                    dve.wait_ge(state_done, 4 * pb + 1)
                    outer(pb, 2)
                    dve.wait_ge(kv_done, 4 * pb + 2)
                    scan(1)
                if n == 6:
                    dve.wait_ge(kv_done, 4 * pb + 3)
                    scan(2)
                    dve.wait_ge(state_done, 4 * pb + 2)
                    outer(pb, 3)
                    dve.wait_ge(kv_done, 4 * pb + 4)
                    scan(3)
                if n == 7:
                    if last:
                        dve.wait_ge(q_done, b)
                        dve.wait_ge(state_done, 4 * b)
                        s = state[:, 3 * 512:4 * 512].rearrange("p (a t) -> p a t", a=2)
                        vec.tensor_tensor(s, s, qT[:, :].unsqueeze(1).broadcast_to((P, 2, T)), ALU.mult)\
                            .then_inc(qs_last, 1)
                        for m in range(4):
                            product_low(vec, dve, pb, m, qs_lo_last)
                    else:
                        for m in range(1, 4):
                            product_low(vec, dve, pb, m, qs_lo_dve)
                if n == 12:
                    dve.wait_ge(wo_ready, b)
                    vec.scalar_tensor_tensor(out=x2T[:, :], in0=r0[:, 0:T], scalar=col[:, C_BO:C_BO + 1],
                                             in1=x_sb[:, bass.ds(pb * T, T)], op0=ALU.add,
                                             op1=ALU.add).then_inc(x2_done, 1)
                if n == 14:
                    dve.wait_ge(s_ready, b)
                    dve.wait_ge(mask_now_done, b)
                    vec.tensor_scalar(cnt_now[:, :], cnt[:, bass.ds(pb * JT, JT)], 1.0, None,
                                      ALU.mult).then_inc(cnt_done, 1)
                    for j in range(JT):
                        vec.tensor_tensor_reduce(mk[:, j * T:(j + 1) * T], r0[:, 0:T],
                                                 mask_now[:, j * T:(j + 1) * T], 1.0, 3e38,
                                                 ALU.add, ALU.min, mxn[:, j:j + 1]).then_inc(masked, 1)
                if n == 17:
                    dve.wait_ge(cnt_done, b)
                    dve.wait_ge(exp_done, JT * pb + JT)
                    st = stepper(rn_step, pb * 2)
                    st(vec.tensor_tensor(rn[:, 0:JT], ssum[:, :], cnt_now[:, :], ALU.mult))
                    st(vec.reciprocal(rn[:, JT:2 * JT], rn[:, 0:JT]))
                    dve.wait_ge(pooled_ready, b)
                    if not last:
                        dve.wait_ge(x2n_sent, 16 * b)
                    for j in range(JT):
                        dst = att[j][:, LAST * W:B * W] if last else stage[:, j * W:(j + 1) * W]
                        vec.tensor_scalar(dst[:, QKV:W], r2[:, j * P:(j + 1) * P], rn[:, JT + j:JT + j + 1],
                                          None, ALU.mult).then_inc(pooled_done, 1)
                if n == UNITS:
                    for j in range(1 if last else JT):
                        store_qkv(b, pb, j, last)

            made = [0]

            def free_slot():
                if made[0] >= 2:
                    dve.wait_ge(sum_dve, made[0] - 1)
                return slot_of(ring_dve, made[0])

            def sum_own(dst, src):
                made[0] += 1
                dve.wait_ge(prod_dve, made[0])
                vec.tensor_reduce(dst, src, AX.X, ALU.add).then_inc(sum_dve, 1)

            def scores(j, t):
                wait_for_qk(dve, j, t)
                slot = free_slot()
                score_products(vec, slot, j, t, prod_dve)
                keys = B if t == LAST else LAST
                sum_own(scores_at(j, t), slot[:, 0:keys * P].rearrange("p (s h d) -> p s h d", h=H, d=DH))

            def batch(b, first=False, last=False):
                for n in range(UNITS + 1):
                    if not first:
                        chain(n, b, b - 1, last)
                    if last:
                        for j, t in EARLY_DVE.get(n, ()):
                            scores(j, t)
                    if n == UNITS:
                        break
                    ahead = not first and n in (6, 9, 10, 11, 14, 15)

                    def low_part():
                        if n >= 1 and not last:
                            h_low(b * UNITS, n - 1)
                        if n == 0 and not first:
                            h_low((b - 1) * UNITS, UNITS - 1)

                    if not first and not last and n - 1 in HIGH_DVE:
                        h_high(b * UNITS, n - 1)
                    if n == 11 and not first:
                        gated_norm(b, b - 1)
                    if ahead and n != 14:
                        low_part()
                    if not first:
                        if n == 9:
                            rstd_begin(b, b - 1)
                        if n == 15:
                            dve.wait_ge(pt_ready, b)
                            vec.tensor_copy(pT[:, :], r1[:, :]).then_inc(pt_done, 1)
                    if not last:
                        hidden_values(b, n)
                        if n == 12:
                            split_x(b + 1)
                    if n == 9 and not first:
                        rstd_end(b - 1)
                    if not ahead or n == 14:
                        low_part()
                    if first and n % 2 == 0 and n // 2 + 1 < NE:
                        gate_low(n // 2 + 1)
                    if first and n % 2 == 1 and (n + 1) // 2 < NE:
                        down_high((n + 1) // 2)
                    if first:
                        setup(n)

            split_x(0)
            gate_low(0)
            down_high(0)
            dve.wait_ge(ld_coef, 32)
            co = coef[:, :].rearrange("p (b e) -> p b e", e=NE)
            step(vec.tensor_scalar(itf[:, :], pr_bc[:, :], -1.0, 1.0, ALU.mult, ALU.add))
            step(vec.tensor_tensor(co[:, :, 0:E], fs_bc[:, :].rearrange("p (b e) -> p b e", e=E),
                                   itf[:, :].unsqueeze(2).broadcast_to((P, B, E)), ALU.mult))
            step(vec.tensor_copy(co[:, :, E:NE], pr_bc[:, :].unsqueeze(2)))
            dve.wait_ge(setup_step, 2)
            batch(0, first=True)
            dve.wait_ge(ld_const, 32)
            with dve.Fori(1, B) as b:
                batch(b)
            batch(B, last=True)

            def softmax(g):
                natural = sc4(g // 2)[:, GT * (g % 2):GT * (g % 2) + GT]
                by_head = natural.rearrange("p t s h -> p t h s")
                n = GT * H
                mx = smx[:, g * n:(g + 1) * n].rearrange("p (t h) -> p t h", h=H)
                sm = ssm[:, g * n:(g + 1) * n].rearrange("p (t h) -> p t h", h=H)
                st = stepper(soft_step, 2 * g)
                dve.wait_ge(sum_dve, made[0])
                if pool_scores_before(g):
                    dve.wait_ge(score_pool, pool_scores_before(g))
                st(vec.tensor_reduce(mx, by_head, AX.X, ALU.max))
                st(vec.tensor_tensor(natural, natural, mx.unsqueeze(2).broadcast_to((P, GT, B, H)), ALU.subtract))
                return natural, by_head, mx, sm

            def softmax_norm(g, natural, by_head, mx, sm):
                st = stepper(norm_step, 2 * g)
                dve.wait_ge(fexp_done, g + 1)
                st(vec.tensor_reduce(sm, by_head, AX.X, ALU.add))
                st(vec.reciprocal(mx, sm))
                vec.tensor_tensor(natural, natural, mx.unsqueeze(2).broadcast_to((P, GT, B, H)),
                                  ALU.mult).then_inc(p_done, 1)

            def values(g):
                dve.wait_ge(p_done, g + 1)
                if g >= 2:
                    dve.wait_ge(atT_ready, g - 1)
                for i in range(GT):
                    if g == 0 and i in TURNED_SUMS:
                        value_products(vec, TURNED_SUMS[i][:, :], g, i, turned_prod)
                    elif i not in POOL_VALUES[g]:
                        slot = free_slot()
                        value_products(vec, slot, g, i, prod_dve)
                        at = (g % 2) * GC + i * P
                        sum_own(atn[:, at:at + P], slot.rearrange("p (s c) -> p c s", c=P))
                sums_until[g] = made[0]

            norm_steps = [0]

            def row_norm(src, dev, off, done, before, normal):
                base = norm_steps[0]
                if base:
                    dve.wait_ge(stat_step, base)
                for t in range(GT):
                    vec.bn_stats(stats[:, t * 6:t * 6 + 6], src[:, t * P:(t + 1) * P]).then_inc(stat_step, 1)
                for t in range(GT):
                    dve.wait_ge(stat_step, base + t + 1)
                    vec.bn_aggr(aggr[:, 2 * t:2 * t + 2], stats[:, t * 6:t * 6 + 6]).then_inc(stat_step, 1)
                base += 2 * GT
                dve.wait_ge(stat_step, base)
                mean, var = (aggr[:, :].rearrange("p (t k) -> p t k", k=2)[:, :, k] for k in range(2))
                r = rsqrt(stepper(stat_step, base), var, LN_EPS, nf, nfi, GT)
                vec.tensor_copy(dev, r).then_inc(done, 1)
                vec.scalar_tensor_tensor(out=off, in0=mean, scalar=-1.0, in1=r, op0=ALU.mult,
                                         op1=ALU.mult).then_inc(done, 1)
                norm_steps[0] = base + RSTEPS
                dve.wait_ge(done, before + 2)
                for t in range(GT // 2, GT):
                    vec.tensor_scalar(src[:, t * P:(t + 1) * P], src[:, t * P:(t + 1) * P], dev[:, t:t + 1],
                                      off[:, t:t + 1], ALU.mult, ALU.add).then_inc(normal, 1)

            def attention_out(g):
                h = hn[:, g * GC:(g + 1) * GC]
                dve.wait_ge(proj_ready, g + 1)
                dve.wait_ge(resid_done, g + 1)
                if g >= 1:
                    dve.wait_ge(dev1_done, 2 * g)
                vec.tensor_tensor(h, pg[1][:, :], resid[:, g * GC:(g + 1) * GC], ALU.add).then_inc(y_done, 1)
                dve.wait_ge(y_done, g + 1)
                k = slice(g * GT, (g + 1) * GT)
                row_norm(h, dev1[:, k], off1[:, k], dev1_done, 2 * g, normal1_dve)

            def h_low_part(g):
                dve.wait_ge(hT_hi_done, g + 1)
                dve.wait_ge(hT_done, g + 1)
                c = slice((g % 2) * GC, (g % 2 + 1) * GC)
                vec.tensor_tensor(hT_lo[:, c], hT[:, c], hT_hi[:, c].bitcast(F32), ALU.subtract).then_inc(hT_lo_done, 1)

            def route(g):
                dve.wait_ge(logit_ready, g + 1)
                st = stepper(route_step, 7 * g)
                l3 = logit[:, :].rearrange("p (t e) -> p t e", e=E)
                st(vec.tensor_tensor(l3, r2[:, 0:GT * E].rearrange("p (t e) -> p t e", e=E),
                                     row_bc[:, R_RB:R_RB + E].unsqueeze(1).broadcast_to((P, GT, E)), ALU.add))
                other = l3.unsqueeze(2).broadcast_to((P, GT, E, E))
                own = l3.unsqueeze(3).broadcast_to((P, GT, E, E))
                gt4 = r_gt[:, :].rearrange("p (t e f) -> p t e f", e=E, f=E)
                eq4 = r_eq[:, :].rearrange("p (t e f) -> p t e f", e=E, f=E)
                eq3 = r_eq[:, :].rearrange("p (t x) -> p t x", t=GT)
                vec.tensor_tensor(gt4, other, own, ALU.is_gt).then_inc(route_gt, 1)
                st(vec.tensor_tensor(eq4, other, own, ALU.is_equal))
                st(vec.tensor_tensor(eq3, eq3, const[:, K_TRI:K_TRI + E * E].unsqueeze(1).broadcast_to((P, GT, E * E)),
                                     ALU.mult))
                dve.wait_ge(route_gt, g + 1)
                st(vec.tensor_tensor(r_gt[:, :], r_gt[:, :], r_eq[:, :], ALU.add))
                st(vec.tensor_reduce(r_rank[:, :], r_gt[:, :].rearrange("p (a f) -> p a f", f=E), AX.X, ALU.add))
                v3 = r_val[:, :].rearrange("p (t e) -> p t e", e=E)
                st(vec.scalar_tensor_tensor(out=v3, in0=r_rank[:, :].rearrange("p (t e) -> p t e", e=E), scalar=2.0,
                                            in1=const[:, K_IDX:K_IDX + E].unsqueeze(1).broadcast_to((P, GT, E)),
                                            op0=ALU.is_lt, op1=ALU.mult))
                st(vec.tensor_reduce(r_max[:, :], v3, AX.X, ALU.max))
                if g >= 1:
                    dve.wait_ge(ohT_ready, g)
                vec.tensor_tensor(onehot[:, :].rearrange("p (t e) -> p t e", e=E), v3,
                                  r_max[:, :].unsqueeze(2).broadcast_to((P, GT, E)),
                                  ALU.is_equal).then_inc(onehot_done, 1)
                dve.wait_ge(onehot_done, g + 1)

            def z_of(g):
                return zf[:, (g % 2) * GC:(g % 2 + 1) * GC]

            def take_sum(g):
                dve.wait_ge(he_used, E * (g + 1))
                dve.wait_ge(h_step, 2 * g + 2)
                if g >= 2:
                    dve.wait_ge(out_sent[g % 2], 16)
                vec.tensor_tensor(z_of(g), (acc, r0)[g % 2][:, :], hn[:, g * GC:(g + 1) * GC], ALU.add).then_inc(z_done, 1)

            def second_norm(g):
                dve.wait_ge(z_done, g + 1)
                dve.wait_ge(dev1_done, 2 * GROUPS)
                if g >= 1:
                    dve.wait_ge(dev2_done, 2 * g)
                k = slice(g * GT, (g + 1) * GT)
                row_norm(z_of(g), dev2[:, k], off2[:, k], dev2_done, 2 * g, normal2_dve)

            def finish_last():
                g = GROUPS - 1
                dve.wait_ge(base_done, GROUPS)
                z3 = z_of(g).rearrange("p (b c) -> p b c", c=P)
                dve.wait_ge(normal2_dve, GT // 2 * GROUPS)
                dve.wait_ge(normal2_done, GT // 2 * GROUPS)
                for t in range(GT):
                    vec.tensor_tensor(z3[:, t], z3[:, t], row_bc[:, R_G2:R_G2 + P], ALU.mult).then_inc(last_step, 1)
                    if t >= 1:
                        dve.wait_ge(last_step, t)
                        vec.tensor_tensor(z3[:, t - 1], z3[:, t - 1], x2_part(g)[:, t - 1], ALU.add).then_inc(last_done, 1)
                dve.wait_ge(last_step, GT)
                vec.tensor_tensor(z3[:, GT - 1], z3[:, GT - 1], x2_part(g)[:, GT - 1], ALU.add).then_inc(last_done, 1)

            scores(0, None)
            store_qkv(B, LAST, 1, True)
            s0 = softmax(0)
            softmax_norm(0, *s0)
            values(0)
            scores(0, LAST)
            s1 = softmax(1)
            attention_out(0)
            softmax_norm(1, *s1)
            h_low_part(0)
            route(0)
            values(1)
            scores(1, 2)
            s2 = softmax(2)
            scores(1, 4)
            softmax_norm(2, *s2)
            attention_out(1)
            s3 = softmax(3)
            h_low_part(1)
            route(1)
            values(2)
            softmax_norm(3, *s3)
            take_sum(0)
            attention_out(2)
            h_low_part(2)
            route(2)
            values(3)
            take_sum(1)
            attention_out(3)
            h_low_part(3)
            route(3)
            second_norm(0)
            second_norm(1)
            take_sum(2)
            second_norm(2)
            take_sum(3)
            second_norm(3)
            finish_last()

        @block.tensor
        def _(pe):
            mmul = nc.tensor.matmul

            def gate_or_up(b, n, first, kind):
                e, half = n // 2, n % 2
                if kind == 0:
                    if n >= 2 or not first:
                        pe.wait_ge(h_done, b * UNITS + n - 1)
                    if n == 0:
                        pe.wait_ge(x_lo_done, b + 1)
                if first and half == 0:
                    pe.wait_ge((w_lo_done, w_lo_pool)[kind], e + 1)
                xh, xl = x_hi[:, bass.ds(b % 2 * T, T)], x_lo[:, bass.ds(b % 2 * T, T)]
                dst = (pg, pu)[kind][n % 2]
                for c in range(2):
                    w = 2 * half + c
                    last = split_matmul(pe, dst[:, c * T:(c + 1) * T], w_part(w_hi, e, kind, w),
                                        w_part(w_lo, e, kind, w), xh, xl, True, True)
                last.then_inc((g_ready, u_ready)[kind], 1)

            def down(before, b, m, first=False):
                e, half = m // 2, m % 2
                pe.wait_ge(lo_done, before + m + 1)
                if first and half == 0:
                    pe.wait_ge(wd_lo_pool, e + 1)
                if m == 0 and not isinstance(b, int):
                    pe.wait_ge(cond_lo, b)
                s = (m % 2) * 2 * T
                for c in range(2):
                    w = 2 * half + c
                    last = split_matmul(pe, acc[:, 0:T], w_part(w_hi, e, 2, w), w_part(w_lo, e, 2, w),
                                        h_hi[:, s + c * T:s + (c + 1) * T], h_lo[:, s + c * T:s + (c + 1) * T],
                                        m == 0 and c == 0, m == UNITS - 1 and c == 1)
                last.then_inc(down_done, 1)

            def project(i, dst):
                return split_matmul(pe, dst, p_hi[:, i * P:(i + 1) * P], p_lo[:, i * P:(i + 1) * P],
                                    c_hi[:, :], c_lo[:, :], True, True)

            def spread_v(m):
                dst = (r2, r0)[m % 2]
                for a in range(2):
                    d = 2 * m + a
                    sel = spread_r[:, d * P:(d + 1) * P]
                    mmul(dst[:, a * T:(a + 1) * T], sel, v_hi[:, :], start=True, stop=False)
                    last = mmul(dst[:, a * T:(a + 1) * T], sel, v_lo[:, :], start=False, stop=True)
                last.then_inc(vb_ready, 1)

            def gather_out(pb, m):
                if isinstance(pb, int):
                    pe.wait_ge(qs_lo_last, m + 1)
                elif m == 0:
                    pe.wait_ge(qs_lo_pool, pb + 1)
                else:
                    pe.wait_ge(qs_lo_dve, 3 * pb + m)
                for a in range(2):
                    d = 2 * m + a
                    sel, c = gather_r[:, d * P:(d + 1) * P], slice(d * T, (d + 1) * T)
                    mmul(r1[:, 0:T], sel, qs_hi[:, c], start=(d == 0), stop=False)
                    last = mmul(r1[:, 0:T], sel, qs_lo[:, c], start=False, stop=(d == DH - 1))
                return last

            def states_out(b, pb):
                pe.wait_ge(gate_done, b)
                for m in range(4):
                    last = gather_out(pb, m)
                last.then_inc(cen_ready, 1)

            def chain(n, b, pb, middle=False):
                if n == 2:
                    pe.wait_ge(cond_lo, b)
                    for i, dst in ((WK // P, r0[:, 0:T]), (WV // P, r0[:, T:2 * T]), (WQ // P, r1[:, 0:T]),
                                   (WGATE // P, r1[:, T:2 * T])):
                        last = project(i, dst)
                    last.then_inc(kvqg_ready, 1)
                if n == 3:
                    pe.wait_ge(v_lo_done, b)
                    pe.wait_ge(k_done, b)
                    spread_v(0)
                    spread_v(1)
                if n == 4:
                    pe.wait_ge(kv_done, 4 * pb + 1)
                    spread_v(2)
                if n == 5:
                    pe.wait_ge(kv_done, 4 * pb + 2)
                    spread_v(3)
                if n == 8:
                    pe.wait_ge(sq_done, b)
                    for j in range(JT):
                        last = mmul(r2[:, j:j + 1], sqT[:, j * P:(j + 1) * P], mean_col[:, :], start=True, stop=True)
                    last.then_inc(var_ready, 1)
                if n == 11 and middle:
                    pe.wait_ge(rstd_step, b * (RSTEPS + JT))
                    mmul(r2[:, T:2 * T], ones[:, :], diag[:, :], start=True, stop=True).then_inc(bc_ready, 1)
                if n == 12 and middle:
                    pe.wait_ge(ln_step, 2 * b)
                    mmul(r0[:, 0:T], projw[:, WO:WO + P], lnT[:, :], start=True, stop=True).then_inc(wo_ready, 1)
                if n == 12 and not middle:
                    pe.wait_ge(x2_done, b)
                    for j in range(JT):
                        last = nc.tensor.transpose(r1[:, j * P:(j + 1) * P], x2T[:, j * P:(j + 1) * P], ident[:, :])
                    last.then_inc(x2t_ready, 1)
                    mmul(r2[0:A, 0:T], projw[:, WPOOL:WPOOL + A], x2T[:, :], start=True, stop=True).then_inc(pre_ready, 1)
                if n == 13:
                    pe.wait_ge(at_done, b)
                    mmul(r0[:, 0:T], nv_rep[0:A, :], atT[0:A, :], start=True, stop=True).then_inc(s_ready, 1)
                if n == 15:
                    pe.wait_ge(exp_done, JT * pb + JT)
                    for j in range(JT):
                        for l in range(JT):
                            last = nc.tensor.transpose(r1[:, l * T + j * P:l * T + (j + 1) * P],
                                                       ex[:, j * T + l * P:j * T + (l + 1) * P], ident[:, :])
                    last.then_inc(pt_ready, 1)
                if n == 16:
                    pe.wait_ge(pt_done, b)
                    for j in range(JT):
                        for l in range(JT):
                            mmul(r2[:, j * P:(j + 1) * P], pT[:, l * T + j * P:l * T + (j + 1) * P],
                                 x2n[:, l * P:(l + 1) * P], start=(l == 0), stop=(l == JT - 1))
                    for l in range(JT):
                        last = mmul(r0[:, 0:T], x2n[:, l * P:(l + 1) * P], pT[:, l * T:(l + 1) * T],
                                    start=(l == 0), stop=(l == JT - 1))
                    last.then_inc(pooled_ready, 1)
                if n == 17:
                    pe.wait_ge(plT_done, b)
                    pe.wait_ge(pooled_done, JT * pb + JT)
                    for j in range(JT):
                        mmul((r1, r2)[j][:, 0:QKV], plT[:, j * P:(j + 1) * P], projw[:, WIN:WIN + QKV],
                             start=True, stop=True).then_inc(qkv_ready, 1)

            def batch(b, first=False, last=False):
                for n in range(UNITS):
                    if not last:
                        gate_or_up(b, n, first, 0)
                    if n == 8 and not first:
                        states_out(b, b - 1)
                    if not last:
                        gate_or_up(b, n, first, 1)
                    if n in (11, 12) and not first:
                        chain(n, b, b - 1, middle=True)
                    if n >= 2 and not last:
                        down(b * UNITS, b, n - 2, first)
                    if n < 2 and not first:
                        down((b - 1) * UNITS, b - 1, UNITS - 2 + n)
                    if not first:
                        chain(n, b, b - 1)

            batch(0, first=True)
            pe.wait_ge(wd_lo_pool, NE)
            pe.wait_ge(p_lo_done, 1)
            pe.wait_ge(spread_done, 1)
            pe.wait_ge(gather_done, 1)
            pe.wait_ge(ld_const, 32)
            with pe.Fori(1, B) as b:
                batch(b)
            batch(B, last=True)

            def turn_values(g):
                if g == 0:
                    for i, products in TURNED_SUMS.items():
                        pe.wait_ge(turned_prod, i + 1)
                        for k in range(B):
                            mmul(pg[0][:, i * P:(i + 1) * P], products[:, k * P:(k + 1) * P], ident[:, :],
                                 start=(k == 0), stop=(k == B - 1))
                pe.wait_ge(sum_dve, sums_until[g])
                pe.wait_ge(sum_pool, sum(len(x) for x in POOL_VALUES[:g + 1]))
                if g >= 1:
                    pe.wait_ge(ctx_done, g)
                for i in range(GT):
                    if g == 0 and i in TURNED_SUMS:
                        continue
                    at = (g % 2) * GC + i * P
                    last = nc.tensor.transpose(pg[0][:, i * P:(i + 1) * P], atn[:, at:at + P], ident[:, :])
                last.then_inc(atT_ready, 1)

            def project_out(g):
                pe.wait_ge(ctx_done, g + 1)
                if g >= 1:
                    pe.wait_ge(y_done, g)
                for i in range(GT):
                    at = (g % 2) * GC + i * P
                    last = mmul(pg[1][:, i * P:(i + 1) * P], ctxT[:, at:at + P], projw[:, WOUT:WOUT + P],
                                start=True, stop=True)
                last.then_inc(proj_ready, 1)

            def turn_h(g):
                if g >= 1:
                    pe.wait_ge(hT_done, g)
                    pe.wait_ge(hT_hi_done, g)
                for k, i in enumerate((2, 0, 3, 1)):
                    pe.wait_ge((normal1_dve, normal1_done)[k % 2], GT // 2 * g + k // 2 + 1)
                    last = nc.tensor.transpose(r1[:, i * P:(i + 1) * P], hn[:, g * GC + i * P:g * GC + (i + 1) * P],
                                               ident[:, :])
                last.then_inc(hT_ready, 1)

            def router(g):
                pe.wait_ge(hT_done, g + 1)
                if g >= 1:
                    pe.wait_ge(ohT_b_done, g)
                    pe.wait_ge(ohT_done, g)
                for i in range(GT):
                    at = (g % 2) * GC + i * P
                    last = mmul(r2[:, i * E:(i + 1) * E], hT[:, at:at + P], projw[:, WROUTE:WROUTE + E],
                                start=True, stop=True)
                last.then_inc(logit_ready, 1)

            def turn_onehot(g):
                pe.wait_ge(onehot_done, g + 1)
                for i in range(GT):
                    last = nc.tensor.transpose(r2[0:E, i * P:(i + 1) * P], onehot[:, i * E:(i + 1) * E], ident[:, :])
                last.then_inc(ohT_ready, 1)

            def expert_in(g, e):
                n = g * E + e
                if n >= 2:
                    pe.wait_ge(gelu_done, n - 1)
                c = slice(e * P, (e + 1) * P)
                own = slice((g % 2) * GC, (g % 2 + 1) * GC)
                if e == 0:
                    pe.wait_ge(hT_lo_done, g + 1)
                split_matmul(pe, pu[n % 2][:, :], w1_hi[:, c], w1_lo[:, c], hT_hi[:, own], hT_lo[:, own], True, False)
                if e:
                    expert_mask(g, e)

            def expert_mask(g, e):
                n = g * E + e
                c = slice(e * P, (e + 1) * P)
                own = slice((g % 2) * GC, (g % 2 + 1) * GC)
                if e == 0:
                    pe.wait_ge(ohT_b_done, g + 1)
                mmul(pu[n % 2][:, :], big_b[0:E, c], ohT_b[0:E, own],
                     start=False, stop=True).then_inc(fpre_ready, 1)

            def expert_out(g, e):
                n = g * E + e
                pe.wait_ge(gelu_done, n + 1)
                for q in range(GT):
                    at = (n % 2) * GC + q * P
                    last = mmul((acc, r0)[g % 2][:, q * P:(q + 1) * P], he[:, at:at + P],
                                w2_sb[:, e * P:(e + 1) * P], start=False, stop=(e == E - 1 and q == GT - 1))
                last.then_inc(he_used, 1)

            def expert_bias(g):
                if g >= 2:
                    pe.wait_ge(z_done, g - 1)
                pe.wait_ge(ohT_done, g + 1)
                for q in range(GT):
                    at = (g % 2) * GC + q * P
                    mmul((acc, r0)[g % 2][:, q * P:(q + 1) * P], ohT[0:E, at:at + P], b2_sb[0:E, :],
                         start=(q == 0), stop=False)

            def between(what, g):
                {"turn_values": turn_values, "project": project_out, "turn_h": turn_h, "router": router,
                 "turn_onehot": turn_onehot}[what](g)

            turn_values(0)
            project_out(0)
            turn_h(0)
            router(0)
            turn_onehot(0)
            pe.wait_ge(w1_lo_done, 1)
            for g in range(GROUPS):
                if g == 0 or not ahead(g - 1):
                    expert_in(g, 0)
                expert_mask(g, 0)
                expert_bias(g)
                for e in range(E):
                    if e + 1 < E:
                        expert_in(g, e + 1)
                    elif ahead(g):
                        expert_in(g + 1, 0)
                    expert_out(g, e)
                    for what, to in BETWEEN.get((g, e), ()):
                        between(what, to)


def bfloat16_bits(constant):
    return (constant.astype(np.float32).view(np.uint32) >> 16).astype(np.uint16)


def shape_constants():
    p, m = np.arange(P)[:, None], np.arange(P)[None, :]
    spread = np.stack([(p == DH * (m // DH) + d) for d in range(DH)], 1).astype(np.float32)
    gather = np.stack([(p // DH == m // DH) & (m % DH == d) for d in range(DH)], 1).astype(np.float32)
    gather -= np.float32(1.0 / P)
    pos = (np.arange(JT)[None, :, None] * P + np.arange(P)[:, None, None])
    l = np.arange(T)[None, None, :]
    masks = bfloat16_bits(np.stack([l > pos, l < pos, l == pos], 1) * BIG)
    consts = np.zeros((P, K_END), np.float32)
    gammas = (1.0 - 2.0 ** (-5.0 - np.arange(H))).repeat(DH)
    consts[:, K_DECAY:K_DECAY + 2 * T] = gammas[:, None]
    consts[:, K_DECAY] = consts[:, K_DECAY + T] = 0.0
    for j in range(JT):
        at = j * P + np.arange(P)
        consts[:, K_CNT + 3 * j], consts[:, K_CNT + 3 * j + 1], consts[:, K_CNT + 3 * j + 2] = at + 1, T - at, T - 1
    consts[:, K_IDX:K_IDX + E] = np.arange(E) + 1
    consts[:, K_TRI:K_TRI + E * E] = (np.arange(E)[None, :] < np.arange(E)[:, None]).reshape(-1)
    big = np.where(np.arange(E)[:, None, None] == np.arange(E)[None, :, None], 0.0, -BIG)
    big = bfloat16_bits(np.broadcast_to(big, (E, E, P)))
    return (spread.reshape(P, -1), gather.reshape(P, -1), np.eye(P, dtype=np.float32), masks.reshape(P, -1),
            consts, np.ascontiguousarray(big).reshape(E, -1))


def kernel(x, fside_Bx8_0, condB_sharedgateprob, itok_B_0_2, **w):
    import concourse.bacc as bacc
    from concourse.bass_utils import run_bass_kernel_spmd

    a = {k: np.asarray(v) for k, v in w.items()}
    gu = [np.concatenate([a["L0_cond_" + n], a["L0_cond_" + s][None]], 0)
          for n, s in (("Wg", "Sg"), ("Wu", "Su"), ("Wd", "Sd"))]
    wd = gu[2].reshape(NE, F // P, P, P).transpose(0, 2, 1, 3).reshape(NE, P, F)
    spread, gather, ident, masks, consts, big = shape_constants()
    arrays = {
        "xT": np.asarray(x).reshape(B * T, P).T,
        "experts": np.concatenate([gu[0], gu[1], wd], 2),
        "proj": np.concatenate([a["L0_attn_Wq"], a["L0_attn_Wk"], a["L0_attn_Wv"], a["L0_attn_Wg"], a["L0_attn_Wo"],
                                a["L0_cond2_W1"], a["L0_ffn_in_proj_w"].T, a["L0_ffn_out_w"].T,
                                a["L0_ffn_router_w"].T], 1),
        "moe_w1": a["L0_ffn_w1"].transpose(2, 0, 1).reshape(P, E * P),
        "moe_w2": a["L0_ffn_w2"].transpose(2, 0, 1).reshape(P, E * P),
        "cols": np.concatenate([a["L0_attn_bg"][:, None], a["L0_attn_bo"][:, None], a["L0_attn_ln_gamma"][:, None],
                                a["L0_attn_ln_beta"][:, None], a["L0_ffn_ln1_g"][:, None], a["L0_ffn_ln1_b"][:, None],
                                a["L0_ffn_b1"].T], 1),
        "small": np.stack([a["L0_cond2_b1"], a["L0_cond2_v"]], 1),
        "rows": np.concatenate([a["L0_ffn_in_proj_b"], a["L0_ffn_out_b"], a["L0_ffn_ln1_g"], a["L0_ffn_ln1_b"],
                                a["L0_ffn_ln2_g"], a["L0_ffn_ln2_b"], a["L0_ffn_router_b"]])[None],
        "moe_b2": a["L0_ffn_b2"],
        "fside": np.asarray(fside_Bx8_0).reshape(1, -1),
        "prob": np.asarray(condB_sharedgateprob).reshape(1, -1),
        "itok": np.asarray(itok_B_0_2).reshape(1, -1),
        "spread": spread, "gather": gather, "ident": ident, "masks": masks, "consts": consts, "big": big,
    }
    arrays = {k: np.ascontiguousarray(v) for k, v in arrays.items()}
    nc = bacc.Bacc("TRN2", target_bir_lowering=False, num_devices=1)
    args = [nc.dram_tensor(k, v.shape, mybir.dt.from_np(v.dtype), kind="ExternalInput").ap()
            for k, v in arrays.items()]
    args.append(nc.dram_tensor("out", (B, T, P), F32, kind="ExternalOutput").ap())
    build(nc, *args)
    return run_bass_kernel_spmd(nc, [arrays], core_ids=[0]).results[0]["out"]
```
